# Optimizing a Trainium2 kernel written in Bass

```python
import numpy as np
import jax
import jax.numpy as jnp

def _softmax(x, axis=-1):
    return jax.nn.softmax(x, axis=axis)

def _gelu(x):
    return jax.nn.gelu(x, approximate=True)

def _silu(x):
    return jax.nn.silu(x)

def _sigmoid(x):
    return jax.nn.sigmoid(x)

def _layernorm(x, axis=-1, eps=1e-05):
    m = jnp.mean(x, axis=axis, keepdims=True)
    v = jnp.var(x, axis=axis, keepdims=True)
    return (x - m) / jnp.sqrt(v + eps)

def _scatter_add(tgt, idx, src, axis=0):
    return tgt.at[idx].add(src)

def _segment_sum(src, seg, n):
    return jax.ops.segment_sum(src, seg, n)
kernel_name = 'mk_dlrm_tower_d1_rec_r8_bdb8f2'

def setup_inputs(seed: int=0):
    np.random.seed(seed)
    _w = jnp.asarray

    def _rec_inputs():
        import jax
        import jax.numpy as jnp
        _tk = jax.random.key(seed)
        dense_ctx = jax.random.normal(jax.random.fold_in(_tk, 190), (1024, 16), jnp.float32)
        ids = jnp.stack([jax.random.randint(jax.random.fold_in(_tk, 200 + f), (1024,), 0, v, jnp.int32) for f, v in enumerate([125000, 1000, 1000, 1000, 1250, 12500, 1250, 12500, 125000, 1250, 1000, 12500, 12500, 1000, 12500, 1250, 1000, 1250, 125000, 12500, 125000, 1250, 12500, 1000])], axis=1)
        tbl_0 = 0.05 * jax.random.normal(jax.random.fold_in(_tk, 500 + 0), (125000, 16), jnp.float32)
        tbl_1 = 0.05 * jax.random.normal(jax.random.fold_in(_tk, 500 + 1), (1000, 16), jnp.float32)
        tbl_2 = 0.05 * jax.random.normal(jax.random.fold_in(_tk, 500 + 2), (1000, 16), jnp.float32)
        tbl_3 = 0.05 * jax.random.normal(jax.random.fold_in(_tk, 500 + 3), (1000, 16), jnp.float32)
        tbl_4 = 0.05 * jax.random.normal(jax.random.fold_in(_tk, 500 + 4), (1250, 16), jnp.float32)
        tbl_5 = 0.05 * jax.random.normal(jax.random.fold_in(_tk, 500 + 5), (12500, 16), jnp.float32)
        tbl_6 = 0.05 * jax.random.normal(jax.random.fold_in(_tk, 500 + 6), (1250, 16), jnp.float32)
        tbl_7 = 0.05 * jax.random.normal(jax.random.fold_in(_tk, 500 + 7), (12500, 16), jnp.float32)
        tbl_8 = 0.05 * jax.random.normal(jax.random.fold_in(_tk, 500 + 8), (125000, 16), jnp.float32)
        tbl_9 = 0.05 * jax.random.normal(jax.random.fold_in(_tk, 500 + 9), (1250, 16), jnp.float32)
        tbl_10 = 0.05 * jax.random.normal(jax.random.fold_in(_tk, 500 + 10), (1000, 16), jnp.float32)
        tbl_11 = 0.05 * jax.random.normal(jax.random.fold_in(_tk, 500 + 11), (12500, 16), jnp.float32)
        tbl_12 = 0.05 * jax.random.normal(jax.random.fold_in(_tk, 500 + 12), (12500, 16), jnp.float32)
        tbl_13 = 0.05 * jax.random.normal(jax.random.fold_in(_tk, 500 + 13), (1000, 16), jnp.float32)
        tbl_14 = 0.05 * jax.random.normal(jax.random.fold_in(_tk, 500 + 14), (12500, 16), jnp.float32)
        tbl_15 = 0.05 * jax.random.normal(jax.random.fold_in(_tk, 500 + 15), (1250, 16), jnp.float32)
        tbl_16 = 0.05 * jax.random.normal(jax.random.fold_in(_tk, 500 + 16), (1000, 16), jnp.float32)
        tbl_17 = 0.05 * jax.random.normal(jax.random.fold_in(_tk, 500 + 17), (1250, 16), jnp.float32)
        tbl_18 = 0.05 * jax.random.normal(jax.random.fold_in(_tk, 500 + 18), (125000, 16), jnp.float32)
        tbl_19 = 0.05 * jax.random.normal(jax.random.fold_in(_tk, 500 + 19), (12500, 16), jnp.float32)
        tbl_20 = 0.05 * jax.random.normal(jax.random.fold_in(_tk, 500 + 20), (125000, 16), jnp.float32)
        tbl_21 = 0.05 * jax.random.normal(jax.random.fold_in(_tk, 500 + 21), (1250, 16), jnp.float32)
        tbl_22 = 0.05 * jax.random.normal(jax.random.fold_in(_tk, 500 + 22), (12500, 16), jnp.float32)
        tbl_23 = 0.05 * jax.random.normal(jax.random.fold_in(_tk, 500 + 23), (1000, 16), jnp.float32)
        _rk = jax.random.fold_in(_tk, 7)
        W_top1 = 0.0693375 * jax.random.normal(jax.random.fold_in(_tk, 801), (208, 512), jnp.float32)
        W_top2 = 0.0441942 * jax.random.normal(jax.random.fold_in(_tk, 802), (512, 256), jnp.float32)
        W_top3 = 0.0625 * jax.random.normal(jax.random.fold_in(_tk, 803), (256, 1), jnp.float32)
        b_top1 = jnp.zeros((512,), jnp.float32)
        b_top2 = jnp.zeros((256,), jnp.float32)
        return (dense_ctx, ids, tbl_0, tbl_1, tbl_2, tbl_3, tbl_4, tbl_5, tbl_6, tbl_7, tbl_8, tbl_9, tbl_10, tbl_11, tbl_12, tbl_13, tbl_14, tbl_15, tbl_16, tbl_17, tbl_18, tbl_19, tbl_20, tbl_21, tbl_22, tbl_23, W_top1, b_top1, W_top2, b_top2, W_top3)
    dense_ctx, ids, tbl_0, tbl_1, tbl_2, tbl_3, tbl_4, tbl_5, tbl_6, tbl_7, tbl_8, tbl_9, tbl_10, tbl_11, tbl_12, tbl_13, tbl_14, tbl_15, tbl_16, tbl_17, tbl_18, tbl_19, tbl_20, tbl_21, tbl_22, tbl_23, W_top1, b_top1, W_top2, b_top2, W_top3 = _rec_inputs()

    def _L0_rec_setup():
        import jax, jax.numpy as jnp
        import numpy as np
        B, F, D = (512, 24, 16)
        LAYER_SIZES = [64, 64, 64]

        def _cin_forward(X0, Ws):
            F_ = X0.shape[1]
            Xk = X0
            outs = []
            for W in Ws:
                H_prev = Xk.shape[1]
                Wr = W.reshape(F_, H_prev, W.shape[1])
                Xk = jnp.einsum('bfd,bhd,fho->bod', X0, Xk, Wr)
                outs.append(Xk.sum(axis=2))
            return jnp.concatenate(outs, axis=1)
        key = jax.random.key(seed)
        k0, k1, k2, k3 = jax.random.split(key, 4)
        X0 = jax.random.normal(k0, (B, F, D), dtype=jnp.float32)
        prev = F
        Ws = []
        for k, h in zip((k1, k2, k3), LAYER_SIZES):
            Ws.append(jax.random.normal(k, (prev * F, h), dtype=jnp.float32) * 0.01)
            prev = h
        return {'X0': X0, 'W0': Ws[0], 'W1': Ws[1], 'W2': Ws[2]}
    _L0_rec_all = _L0_rec_setup()
    _L0_rec_in = {k: v for k, v in _L0_rec_all.items() if k in ('W0', 'W1', 'W2')}
    del _L0_rec_all
    return {'dense_ctx': dense_ctx, 'ids': ids, 'tbl_0': tbl_0, 'tbl_1': tbl_1, 'tbl_2': tbl_2, 'tbl_3': tbl_3, 'tbl_4': tbl_4, 'tbl_5': tbl_5, 'tbl_6': tbl_6, 'tbl_7': tbl_7, 'tbl_8': tbl_8, 'tbl_9': tbl_9, 'tbl_10': tbl_10, 'tbl_11': tbl_11, 'tbl_12': tbl_12, 'tbl_13': tbl_13, 'tbl_14': tbl_14, 'tbl_15': tbl_15, 'tbl_16': tbl_16, 'tbl_17': tbl_17, 'tbl_18': tbl_18, 'tbl_19': tbl_19, 'tbl_20': tbl_20, 'tbl_21': tbl_21, 'tbl_22': tbl_22, 'tbl_23': tbl_23, 'W_top1': W_top1, 'b_top1': b_top1, 'W_top2': W_top2, 'b_top2': b_top2, 'W_top3': W_top3, 'L0_rec_W0': _L0_rec_in['W0'], 'L0_rec_W1': _L0_rec_in['W1'], 'L0_rec_W2': _L0_rec_in['W2']}

def reference(dense_ctx, ids, tbl_0, tbl_1, tbl_2, tbl_3, tbl_4, tbl_5, tbl_6, tbl_7, tbl_8, tbl_9, tbl_10, tbl_11, tbl_12, tbl_13, tbl_14, tbl_15, tbl_16, tbl_17, tbl_18, tbl_19, tbl_20, tbl_21, tbl_22, tbl_23, W_top1, b_top1, W_top2, b_top2, W_top3, L0_rec_W0, L0_rec_W1, L0_rec_W2):
    import jax
    import jax.numpy as jnp

    def _L0_rec_ref(X0, W0, W1, W2):
        import jax, jax.numpy as jnp
        import numpy as np
        B, F, D = (512, 24, 16)
        LAYER_SIZES = [64, 64, 64]

        def _cin_forward(X0, Ws):
            F_ = X0.shape[1]
            Xk = X0
            outs = []
            for W in Ws:
                H_prev = Xk.shape[1]
                Wr = W.reshape(F_, H_prev, W.shape[1])
                Xk = jnp.einsum('bfd,bhd,fho->bod', X0, Xk, Wr)
                outs.append(Xk.sum(axis=2))
            return jnp.concatenate(outs, axis=1)
        return _cin_forward(X0, (W0, W1, W2))
    e = jnp.stack([tbl_0[ids[:, 0]], tbl_1[ids[:, 1]], tbl_2[ids[:, 2]], tbl_3[ids[:, 3]], tbl_4[ids[:, 4]], tbl_5[ids[:, 5]], tbl_6[ids[:, 6]], tbl_7[ids[:, 7]], tbl_8[ids[:, 8]], tbl_9[ids[:, 9]], tbl_10[ids[:, 10]], tbl_11[ids[:, 11]], tbl_12[ids[:, 12]], tbl_13[ids[:, 13]], tbl_14[ids[:, 14]], tbl_15[ids[:, 15]], tbl_16[ids[:, 16]], tbl_17[ids[:, 17]], tbl_18[ids[:, 18]], tbl_19[ids[:, 19]], tbl_20[ids[:, 20]], tbl_21[ids[:, 21]], tbl_22[ids[:, 22]], tbl_23[ids[:, 23]]], axis=1)
    z = _L0_rec_ref(e, L0_rec_W0, L0_rec_W1, L0_rec_W2)
    z = z.reshape(z.shape[0], -1)
    h = jnp.concatenate([z, dense_ctx], axis=1)
    h = jnp.maximum(h @ W_top1 + b_top1, 0.0)
    h = jnp.maximum(h @ W_top2 + b_top2, 0.0)
    y = h @ W_top3
    return y

_drawn_inputs = setup_inputs


def setup_inputs(seed=0):
    import zlib

    import numpy as np

    out = dict(_drawn_inputs(seed))
    spreads = {'b_top1': (0.0, 0.1), 'b_top2': (0.0, 0.1)}
    factors = {'tbl_0': 8.0,
     'tbl_1': 8.0,
     'tbl_2': 8.0,
     'tbl_3': 8.0,
     'tbl_4': 8.0,
     'tbl_5': 8.0,
     'tbl_6': 8.0,
     'tbl_7': 8.0,
     'tbl_8': 8.0,
     'tbl_9': 8.0,
     'tbl_10': 8.0,
     'tbl_11': 8.0,
     'tbl_12': 8.0,
     'tbl_13': 8.0,
     'tbl_14': 8.0,
     'tbl_15': 8.0,
     'tbl_16': 8.0,
     'tbl_17': 8.0,
     'tbl_18': 8.0,
     'tbl_19': 8.0,
     'tbl_20': 8.0,
     'tbl_21': 8.0,
     'tbl_22': 8.0,
     'tbl_23': 8.0,
     'L0_rec_W0': 8.0,
     'L0_rec_W1': 8.0,
     'L0_rec_W2': 8.0}
    for name, (base, spread) in spreads.items():
        noise = np.random.default_rng([zlib.crc32(name.encode()), seed]).standard_normal(out[name].shape)
        drawn = base * np.exp(spread * noise) if base else spread * noise
        out[name] = jnp.asarray(drawn.astype(out[name].dtype))
    for name, factor in factors.items():
        out[name] = (out[name] * factor).astype(out[name].dtype)
    return out
```

```python
from contextlib import ExitStack

import numpy as np

import concourse.bass as bass
from concourse import mybir

F32 = mybir.dt.float32
F32R = mybir.dt.float32r
I32 = mybir.dt.int32
ALU = mybir.AluOpType
ACT = mybir.ActivationFunctionType

P = 128
BATCH, FEATURES, DIM, HIDDEN = 1024, 24, 16, 64
TILES = BATCH // P
CHUNK = 512
PAIR = 2 * CHUNK
COLUMNS = DIM * P
FB, HB = 8, 16
NI, NJ = FEATURES // FB, HIDDEN // HB
RING = 2
GROUP = P // DIM
GROUPS = P // GROUP
BATCHES = 4
PER_BATCH = GROUPS // BATCHES
HALF_F = FEATURES // 2
SLOTS = HALF_F + 1
TOP1, TOP2 = 512, 256
N_DENSE = 16
M1, M2 = TOP1 // P, TOP2 // P


def dlrm_cin_tower(nc, ids, tables, w0, w0_mirror, w1, w2, top1, top1_bias, top2, top2_bias, top3,
                   dense_t, identity, select_h, same_sample, out):
    with ExitStack() as ctx:
        def sb(name, shape, dtype=F32):
            return ctx.enter_context(nc.sbuf_tensor(name, shape, dtype))

        def ps(name, shape):
            return ctx.enter_context(nc.psum_tensor(name, shape, F32))

        def sem(name):
            return ctx.enter_context(nc.semaphore(name))

        x0_rows = nc.dram_tensor("x0_rows", [TILES, (FEATURES + FB) * DIM, P], F32, kind="Internal").ap()
        x0_groups = nc.dram_tensor("x0_groups", [TILES, P, DIM, FEATURES], F32, kind="Internal").ap()
        x0_f = x0_rows.rearrange("s (f d) b -> s f (d b)", d=DIM)

        ids_all = sb("ids_all", [P, TILES, FEATURES], I32)
        ids_tile = sb("ids_tile", [P, FEATURES], I32)
        embedded = sb("embedded", [P, FEATURES * DIM])
        x0_t = sb("x0_t", [P, NI, P])
        x0_by_f = sb("x0_by_f", [P, 2, NI, PAIR])
        x0_by_g = sb("x0_by_g", [P, 2, NI, PAIR])
        x1_split = sb("x1_split", [P, 2, PAIR], F32R)
        products = sb("products", [P, RING, NI, PAIR])
        embedded_df = sb("embedded_df", [P, DIM, FEATURES])
        x2 = sb("x2", [HIDDEN, P, DIM])
        grouped_x2 = sb("grouped_x2", [P, GROUPS, HIDDEN])
        grouped_x0 = sb("grouped_x0", [P, GROUPS, FEATURES])
        block_x0 = sb("block_x0", [P, GROUPS, 2, SLOTS, GROUP])
        inter = sb("inter", [P, SLOTS, BATCH])
        z1_a = sb("z1_a", [P, CHUNK])
        z1_b = sb("z1_b", [P, 2 * P])
        z1_c = sb("z1_c", [P, P])
        z1 = sb("z1", [P, BATCH])
        w0_sb = sb("w0_sb", [P, NI, HIDDEN])
        w0_mirror_sb = sb("w0_mirror_sb", [P, NI, HIDDEN])
        w1_sb = sb("w1_sb", [P, NJ, NI, HIDDEN])
        w2_sb = sb("w2_sb", [P, HALF_F, HIDDEN])
        top1_z1 = sb("top1_z1", [P, TOP1])
        top1_z23 = sb("top1_z23", [P, TOP1])
        top1_dense = sb("top1_dense", [N_DENSE, TOP1])
        top2_sb = sb("top2_sb", [P, M1, TOP2])
        top3_sb = sb("top3_sb", [P, M2])
        bias1 = sb("bias1", [P, M1])
        bias2 = sb("bias2", [P, M2])
        dense_sb = sb("dense_sb", [N_DENSE, BATCH])
        ident = sb("ident", [P, P])
        select_f32 = sb("select_f32", [P, NJ, P])
        select = sb("select", [P, NJ, P], F32R)
        sample_mask = sb("sample_mask", [P, GROUP])
        y_row = sb("y_row", [1, BATCH])

        x1_by_h = ps("x1_by_h", [P, 2, PAIR])
        x1_ps = ps("x1_ps", [P, CHUNK])
        x2_ps = ps("x2_ps", [P, CHUNK])
        group_ps = ps("group_ps", [P, 2, CHUNK])

        spare = x0_by_f[:].rearrange("p a b c -> p (a b c)")
        hidden1 = spare[:, 0:M1 * BATCH].rearrange("p (m b) -> p m b", m=M1)
        hidden2 = spare[:, M1 * BATCH:(M1 + M2) * BATCH].rearrange("p (m b) -> p m b", m=M2)

        loaded = sem("loaded")
        gathered = sem("gathered")
        ids_ready = sem("ids_ready")
        x0_transposed = sem("x0_transposed")
        x0_t_copied = sem("x0_t_copied")
        x0_permuted = sem("x0_permuted")
        x0_stored = sem("x0_stored")
        by_f_loaded = [sem("by_f_loaded_0"), sem("by_f_loaded_1")]
        by_g_loaded = [sem("by_g_loaded_0"), sem("by_g_loaded_1")]
        x0_grouped = sem("x0_grouped")
        w0_ready = sem("w0_ready")
        select_ready = sem("select_ready")
        squares_made = sem("squares_made")
        x1_made = sem("x1_made")
        x1_high = sem("x1_high")
        x1_low = sem("x1_low")
        x1_spread = sem("x1_spread")
        products_made = sem("products_made")
        products_used = sem("products_used")
        x2_copied = sem("x2_copied")
        group_made = sem("group_made")
        group_copied = sem("group_copied")
        block_ready = sem("block_ready")
        z1_step = sem("z1_step")
        z3_made = sem("z3_made")
        z3_copied = sem("z3_copied")
        mlp_made = sem("mlp_made")
        mlp_copied = sem("mlp_copied")
        stored = sem("stored")
        pe_passed, pool_passed = sem("pe_passed"), sem("pool_passed")

        N_LOADS = 16
        LOADED = 16 * 17
        block = ctx.enter_context(nc.Block())

        @block.sync
        def _(sp):
            for dst, src in (
                (ids_all[:], ids.rearrange("s p f -> p s f")),
                (ident[:], identity), (w0_sb[:], w0), (w0_mirror_sb[:], w0_mirror),
                (select_f32[:], select_h), (w1_sb[:], w1), (sample_mask[:], same_sample),
                (w2_sb[:], w2), (top1_z1[0:HIDDEN, :], top1[0:HIDDEN, :]),
                (top1_z1[HIDDEN:P, :], top1[0:HIDDEN, :]),
                (top1_z23[:], top1[HIDDEN:3 * HIDDEN, :]),
                (top1_dense[:], top1[3 * HIDDEN:3 * HIDDEN + N_DENSE, :]),
                (top2_sb[:], top2.rearrange("(k p) n -> p k n", p=P)), (top3_sb[:], top3),
                (bias1[:], top1_bias), (bias2[:], top2_bias), (dense_sb[:], dense_t),
            ):
                sp.dma_start(dst, src).then_inc(loaded, 16)

            def tile(s, first=False):
                sp.wait_ge(x0_t_copied, s + 1)
                sp.wait_ge(x0_permuted, s + 1)
                sp.dma_start(x0_rows[s, 0:FEATURES * DIM, :].rearrange("(i p) b -> p i b", p=P),
                             x0_t[:]).then_inc(x0_stored, 16)
                sp.dma_start(x0_rows[s, FEATURES * DIM:, :], x0_t[:, 0, :]).then_inc(x0_stored, 16)
                sp.dma_start(x0_groups[s], embedded_df[:]).then_inc(x0_stored, 16)
                sp.wait_ge(x0_stored, 48 * s + 48)
                for c in range(2):
                    cols = slice(c * PAIR, (c + 1) * PAIR)
                    if not first:
                        sp.wait_ge(x1_made, 2 * s - 1 + c)
                    for i in range(NI):
                        sp.dma_start(x0_by_g[:, c, i, :],
                                     x0_f[s, FB * i:FB * i + HB, cols].unsqueeze(1).broadcast_to([HB, FB, PAIR])
                                     ).then_inc(by_g_loaded[c], 16)
                    if not first:
                        sp.wait_ge(products_made, 8 * s - 4 + 4 * c)
                    for i in range(NI):
                        sp.dma_start(x0_by_f[:, c, i, :],
                                     x0_f[s, FB * i:FB * i + FB, cols].unsqueeze(0).broadcast_to([HB, FB, PAIR])
                                     ).then_inc(by_f_loaded[c], 16)

            tile(0, first=True)
            with sp.Fori(1, TILES) as s:
                tile(s)
            sp.wait_ge(mlp_copied, 2 * M1 + 2 * M2 + 2)
            sp.dma_start(out.rearrange("b o -> o b"), y_row[:]).then_inc(stored, 16)
            sp.wait_ge(stored, 16)

        @block.gpsimd
        def _(pool):
            def copy_ids(s):
                nc.gpsimd.tensor_copy(ids_tile[:], ids_all[:, s, :]).then_inc(ids_ready, 1)
                pool.wait_ge(ids_ready, s + 1)
                pool.sem_inc(pool_passed, 1)

            def gather(features):
                for f in features:
                    nc.gpsimd.indirect_dma_start(
                        out=embedded[:, f * DIM:(f + 1) * DIM], out_offset=None, in_=tables[f],
                        in_offset=bass.IndirectOffsetOnAxis(ap=ids_tile[:, f:f + 1], axis=0),
                    ).then_inc(gathered, 16)

            def sum_d(s, c):
                part = x1_split[:, c, :].bitcast(F32)
                total = z1[:, bass.ts(s, P)]
                pool.wait_ge(x1_high, 4 * s + 2 * c + 2)
                pool.wait_ge(x1_low, 4 * s + 2 * c + 2)
                done = 7 * s + 3 * c
                if not (isinstance(s, int) and s + c == 0):
                    pool.wait_ge(z1_step, done)
                nc.gpsimd.tensor_tensor(z1_a[:], part[:, 0:CHUNK], part[:, CHUNK:PAIR],
                                        ALU.add).then_inc(z1_step, 1)
                pool.wait_ge(z1_step, done + 1)
                nc.gpsimd.tensor_tensor(z1_b[:], z1_a[:, 0:2 * P], z1_a[:, 2 * P:4 * P],
                                        ALU.add).then_inc(z1_step, 1)
                pool.wait_ge(z1_step, done + 2)
                if c == 0:
                    nc.gpsimd.tensor_tensor(total, z1_b[:, 0:P], z1_b[:, P:2 * P],
                                            ALU.add).then_inc(z1_step, 1)
                else:
                    nc.gpsimd.tensor_tensor(z1_c[:], z1_b[:, 0:P], z1_b[:, P:2 * P],
                                            ALU.add).then_inc(z1_step, 1)
                    pool.wait_ge(z1_step, done + 3)
                    nc.gpsimd.tensor_tensor(total, total, z1_c[:], ALU.add).then_inc(z1_step, 1)

            half = FEATURES // 2
            pool.wait_ge(loaded, LOADED)
            copy_ids(0)
            gather(range(FEATURES))
            pool.wait_ge(x0_transposed, 1)
            pool.wait_ge(x0_permuted, 1)
            copy_ids(1)
            gather(range(FEATURES))
            sum_d(0, 0)
            with pool.Fori(1, TILES - 1) as s:
                pool.wait_ge(x0_transposed, s + 1)
                pool.wait_ge(x0_permuted, s + 1)
                copy_ids(s + 1)
                gather(range(half))
                sum_d(s - 1, 1)
                gather(range(half, FEATURES))
                sum_d(s, 0)
            sum_d(TILES - 2, 1)
            sum_d(TILES - 1, 0)
            sum_d(TILES - 1, 1)

        @block.tensor
        def _(pe):
            def transpose_x0(s):
                pe.wait_ge(gathered, 16 * FEATURES * s + 16 * FEATURES)
                for i in range(NI):
                    mm = nc.tensor.transpose(x1_ps[:, i * P:(i + 1) * P], embedded[:, i * P:(i + 1) * P], ident[:])
                mm.then_inc(x0_transposed, 1)

            def layer1(s, c):
                pe.wait_ge(squares_made, 2 * s + c + 1)
                for i in range(NI):
                    for u in range(2):
                        mm = nc.tensor.matmul(x1_ps[u * HIDDEN:(u + 1) * HIDDEN, :], w0_sb[:, i, :],
                                              x0_by_g[:, c, i, u * CHUNK:(u + 1) * CHUNK],
                                              start=(i == 0), stop=(i == NI - 1))
                mm.then_inc(x1_made, 1)

            def spread_x1(s, c, j):
                n = 8 * s + 4 * c + j
                if not (isinstance(s, int) and n < 2):
                    pe.wait_ge(products_made, n - 1)
                if j == 0:
                    pe.wait_ge(x1_high, 4 * s + 2 * c + 2)
                    pe.wait_ge(x1_low, 4 * s + 2 * c + 2)
                for u in range(2):
                    cols = slice(u * CHUNK, (u + 1) * CHUNK)
                    mm = nc.tensor.matmul(x1_by_h[:, j % 2, cols], select[:, j, :], x1_split[:, c, cols],
                                          start=True, stop=True)
                mm.then_inc(x1_spread, 1)

            def layer2(s, c, j):
                pe.wait_ge(products_made, 8 * s + 4 * c + j + 1)
                if j == 0 and not (isinstance(s, int) and 2 * s + c == 0):
                    pe.wait_ge(x2_copied, 4 * s + 2 * c)
                for i in range(NI):
                    for u in range(2):
                        mm = nc.tensor.matmul(x2_ps[u * HIDDEN:(u + 1) * HIDDEN, :], w1_sb[:, j, i, :],
                                              products[:, j % RING, i, u * CHUNK:(u + 1) * CHUNK],
                                              start=(j == 0 and i == 0), stop=(j == NJ - 1 and i == NI - 1))
                mm.then_inc(products_used, 1)

            def group_bank(s, m):
                pe.wait_ge(group_copied, 8 * s + m + 1)
                return group_ps[:, m % 2, :]

            def transpose_groups(s, k):
                bank = group_bank(s, k)
                if k == 0:
                    pe.wait_ge(x2_copied, 4 * s + 4)
                pe.sem_inc(pe_passed, 1)
                columns = x2[:].rearrange("r (g b) d -> r g (b d)", b=GROUP)
                for n in range(PER_BATCH):
                    mm = nc.tensor.transpose(bank[:, n * HIDDEN:(n + 1) * HIDDEN],
                                             columns[:, k * PER_BATCH + n, :], ident[0:HIDDEN, 0:HIDDEN])
                mm.then_inc(group_made, 1)

            def interact_groups(s, k):
                bank = group_bank(s, BATCHES + k)
                pe.wait_ge(block_ready, 8 * s + 9)
                width = SLOTS * GROUP
                for n in range(PER_BATCH):
                    g = k * PER_BATCH + n
                    for half in range(2):
                        mm = nc.tensor.matmul(bank[half * HIDDEN:(half + 1) * HIDDEN, n * width:(n + 1) * width],
                                              grouped_x2[:, g, :],
                                              block_x0[:, g, half, :, :],
                                              start=True, stop=True)
                mm.then_inc(group_made, 1)

            def tile(s, first=False, last=False):
                spread_x1(s, 0, 2)
                layer2(s, 0, 0)
                if not last:
                    transpose_x0(s + 1)
                if not first:
                    transpose_groups(s - 1, 0)
                    transpose_groups(s - 1, 1)
                spread_x1(s, 0, 3)
                layer2(s, 0, 1)
                if not last:
                    pe.wait_ge(x0_t_copied, s + 2)
                layer1(s, 1)
                if not first:
                    transpose_groups(s - 1, 2)
                    transpose_groups(s - 1, 3)
                layer2(s, 0, 2)
                spread_x1(s, 1, 0)
                spread_x1(s, 1, 1)
                layer2(s, 0, 3)
                spread_x1(s, 1, 2)
                layer2(s, 1, 0)
                if not first:
                    interact_groups(s - 1, 0)
                    interact_groups(s - 1, 1)
                spread_x1(s, 1, 3)
                layer2(s, 1, 1)
                if not last:
                    layer1(s + 1, 0)
                layer2(s, 1, 2)
                if not first:
                    interact_groups(s - 1, 2)
                if not last:
                    spread_x1(s + 1, 0, 0)
                    spread_x1(s + 1, 0, 1)
                layer2(s, 1, 3)
                if not first:
                    interact_groups(s - 1, 3)

            pe.wait_ge(loaded, LOADED)
            transpose_x0(0)
            pe.wait_ge(w0_ready, 1)
            pe.wait_ge(select_ready, 1)
            pe.wait_ge(x0_t_copied, 1)
            layer1(0, 0)
            spread_x1(0, 0, 0)
            spread_x1(0, 0, 1)
            tile(0, first=True)
            with pe.Fori(1, TILES - 1) as s:
                tile(s)
            tile(TILES - 1, last=True)
            for k in range(BATCHES):
                transpose_groups(TILES - 1, k)
            for k in range(BATCHES):
                interact_groups(TILES - 1, k)

            pe.wait_ge(group_copied, 8 * TILES + 2)
            for t in range(HALF_F):
                for u in range(2):
                    mm = nc.tensor.matmul(x2_ps[u * HIDDEN:(u + 1) * HIDDEN, :], w2_sb[:, t, :],
                                          inter[:, 1 + t, u * CHUNK:(u + 1) * CHUNK],
                                          start=(t == 0), stop=(t == HALF_F - 1))
            mm.then_inc(z3_made, 1)

            def bank(n):
                if n >= 4:
                    pe.wait_ge(mlp_copied, n - 3)
                return x1_by_h[:, (n // 2) % 2, (n % 2) * CHUNK:(n % 2 + 1) * CHUNK]

            pe.wait_ge(z1_step, 7 * TILES)
            pe.wait_ge(z3_copied, 2)
            n = 0
            for u in range(2):
                cols = slice(u * CHUNK, (u + 1) * CHUNK)
                for m in range(M1):
                    to, units = bank(n), slice(m * P, (m + 1) * P)
                    nc.tensor.matmul(to, top1_z1[:, units], z1[:, cols], start=True, stop=False)
                    nc.tensor.matmul(to, top1_dense[:, units], dense_sb[:, cols], start=False, stop=False)
                    nc.tensor.matmul(to, top1_z23[:, units], inter[:, 0, cols],
                                     start=False, stop=True).then_inc(mlp_made, 1)
                    n += 1
            for u in range(2):
                cols = slice(u * CHUNK, (u + 1) * CHUNK)
                pe.wait_ge(mlp_copied, M1 * (u + 1))
                for m in range(M2):
                    to, units = bank(n), slice(m * P, (m + 1) * P)
                    for k in range(M1):
                        mm = nc.tensor.matmul(to, top2_sb[:, k, units], hidden1[:, k, cols],
                                              start=(k == 0), stop=(k == M1 - 1))
                    mm.then_inc(mlp_made, 1)
                    n += 1
            for u in range(2):
                cols = slice(u * CHUNK, (u + 1) * CHUNK)
                to = bank(n)
                pe.wait_ge(mlp_copied, 2 * M1 + M2 * (u + 1))
                for k in range(M2):
                    mm = nc.tensor.matmul(to[0:1, :], top3_sb[:, k:k + 1], hidden2[:, k, cols],
                                          start=(k == 0), stop=(k == M2 - 1))
                mm.then_inc(mlp_made, 1)
                n += 1

        @block.vector
        def _(dve):
            def square(s, c):
                dve.wait_ge(by_f_loaded[c], 48 * s + 48)
                dve.wait_ge(by_g_loaded[c], 48 * s + 48)
                nc.vector.tensor_tensor(x0_by_g[:, c], x0_by_f[:, c], x0_by_g[:, c],
                                        ALU.mult).then_inc(squares_made, 1)

            def product(s, c, j):
                n = 8 * s + 4 * c + j
                dve.wait_ge(x1_spread, n + 1)
                if not (isinstance(s, int) and n < RING):
                    dve.wait_ge(products_used, n + 1 - RING)
                spread = x1_by_h[:, j % 2, :].unsqueeze(1).broadcast_to([P, NI, PAIR])
                nc.vector.tensor_tensor(products[:, j % RING], x0_by_f[:, c], spread,
                                        ALU.mult).then_inc(products_made, 1)

            def low_part(s, c):
                dve.wait_ge(x1_high, 4 * s + 2 * c + 2)
                for u in range(2):
                    here, there = slice(u * HIDDEN, (u + 1) * HIDDEN), slice((1 - u) * HIDDEN, (2 - u) * HIDDEN)
                    cols = slice(u * CHUNK, (u + 1) * CHUNK)
                    nc.vector.tensor_tensor(x1_split[there, c, cols], x1_ps[here, :], x1_split[here, c, cols],
                                            ALU.subtract).then_inc(x1_low, 1)

            def pair(s, c, nxt):
                product(s, c, 0)
                product(s, c, 1)
                if nxt is not None:
                    square(*nxt)
                product(s, c, 2)
                if nxt is not None:
                    low_part(*nxt)
                product(s, c, 3)

            dve.wait_ge(loaded, LOADED)
            nc.vector.tensor_tensor(w0_sb[HIDDEN:P], w0_sb[HIDDEN:P], w0_mirror_sb[HIDDEN:P],
                                    ALU.add).then_inc(w0_ready, 1)
            nc.vector.tensor_copy(select[:], select_f32[:]).then_inc(select_ready, 1)
            square(0, 0)
            low_part(0, 0)
            pair(0, 0, (0, 1))
            pair(0, 1, (1, 0))
            with dve.Fori(1, TILES - 1) as s:
                pair(s, 0, (s, 1))
                pair(s, 1, (s + 1, 0))
            pair(TILES - 1, 0, (TILES - 1, 1))
            pair(TILES - 1, 1, None)

        @block.scalar
        def _(act):
            def copy_x0(s):
                act.wait_ge(gathered, 16 * FEATURES * s + 16 * FEATURES)
                if not (isinstance(s, int) and s == 0):
                    act.wait_ge(x0_stored, 48 * s)
                nc.scalar.activation(embedded_df[:], embedded[:].rearrange("p (f d) -> p d f", d=DIM),
                                     ACT.Copy).then_inc(x0_permuted, 1)
                act.wait_ge(x0_transposed, s + 1)
                nc.scalar.activation(x0_t[:], x1_ps[:, 0:NI * P].rearrange("p (i b) -> p i b", i=NI),
                                     ACT.Copy).then_inc(x0_t_copied, 1)

            def high_part(s, c):
                act.wait_ge(x1_made, 2 * s + c + 1)
                if not (isinstance(s, int) and s == 0):
                    act.wait_ge(z1_step, 7 * s - 4 + 4 * c)
                    act.wait_ge(x1_spread, 8 * s - 4 + 4 * c)
                for u in range(2):
                    rows, cols = slice(u * HIDDEN, (u + 1) * HIDDEN), slice(u * CHUNK, (u + 1) * CHUNK)
                    nc.scalar.activation(x1_split[rows, c, cols], x1_ps[rows, :],
                                         ACT.Copy).then_inc(x1_high, 1)

            def copy_x2(s, c):
                act.wait_ge(products_used, 8 * s + 4 * c + 4)
                if c == 0 and not (isinstance(s, int) and s == 0):
                    act.wait_ge(group_made, 8 * s - 4)
                for u in range(2):
                    d0, dims = 8 * c + 4 * u, CHUNK // P
                    nc.scalar.activation(x2[:, :, d0:d0 + dims].rearrange("r b d -> r d b"),
                                         x2_ps[u * HIDDEN:(u + 1) * HIDDEN, :].rearrange("r (d b) -> r d b", d=dims),
                                         ACT.Copy).then_inc(x2_copied, 1)

            def copy_grouped(s, k):
                act.wait_ge(group_made, 8 * s + k + 1)
                nc.scalar.activation(grouped_x2[:, k * PER_BATCH:(k + 1) * PER_BATCH, :],
                                     group_ps[:, k % 2, 0:PER_BATCH * HIDDEN].rearrange(
                                         "p (n r) -> p n r", n=PER_BATCH),
                                     ACT.Copy).then_inc(group_copied, 1)

            def block_diagonal(s, samples):
                act.wait_ge(x0_grouped, 16 * s + 16)
                for b in samples:
                    for half in range(2):
                        ins = nc.scalar.activation(
                            block_x0[:, :, half, 1:SLOTS, b],
                            grouped_x0[:, :, half * HALF_F:(half + 1) * HALF_F],
                            ACT.Copy, scale=sample_mask[:, b:b + 1])
                    ins.then_inc(block_ready, 1)

            def load_groups(s, first=False):
                act.wait_ge(x0_stored, 48 * s + 48)
                if not first:
                    act.wait_ge(block_ready, 8 * s + 1)
                act.dma_start(grouped_x0[:], x0_groups[s].rearrange("(g b) d f -> (b d) g f", b=GROUP)
                              ).then_inc(x0_grouped, 16)

            def copy_interactions(s, k):
                act.wait_ge(group_made, 8 * s + BATCHES + k + 1)
                samples = inter[:, :, bass.ds(s * P + k * PER_BATCH * GROUP, PER_BATCH * GROUP)]
                nc.scalar.activation(
                    samples.rearrange("p t (n b) -> p t n b", n=PER_BATCH),
                    group_ps[:, k % 2, 0:PER_BATCH * SLOTS * GROUP].rearrange(
                        "p (n t b) -> p t n b", n=PER_BATCH, t=SLOTS),
                    ACT.Copy).then_inc(group_copied, 1)

            def tile(s, first=False, last=False):
                if not last:
                    copy_x0(s + 1)
                if not first:
                    copy_grouped(s - 1, 0)
                    copy_grouped(s - 1, 1)
                high_part(s, 1)
                if not first:
                    copy_grouped(s - 1, 2)
                    copy_grouped(s - 1, 3)
                    block_diagonal(s - 1, range(GROUP // 2))
                copy_x2(s, 0)
                if not first:
                    block_diagonal(s - 1, range(GROUP // 2, GROUP))
                load_groups(s, first)
                if not first:
                    copy_interactions(s - 1, 0)
                    copy_interactions(s - 1, 1)
                if not last:
                    high_part(s + 1, 0)
                if not first:
                    copy_interactions(s - 1, 2)
                copy_x2(s, 1)
                if not first:
                    copy_interactions(s - 1, 3)

            act.wait_ge(loaded, LOADED)
            act.sem_inc(group_copied, 2)
            for half in range(2):
                ins = nc.scalar.activation(block_x0[:, :, half, 0, :],
                                           sample_mask[:].unsqueeze(1).broadcast_to([P, GROUPS, GROUP]), ACT.Copy)
            ins.then_inc(block_ready, 1)
            copy_x0(0)
            high_part(0, 0)
            tile(0, first=True)
            with act.Fori(1, TILES - 1) as s:
                tile(s)
            tile(TILES - 1, last=True)
            for k in range(BATCHES):
                copy_grouped(TILES - 1, k)
            block_diagonal(TILES - 1, range(GROUP))
            for k in range(BATCHES):
                copy_interactions(TILES - 1, k)

            act.wait_ge(z3_made, 1)
            for u in range(2):
                nc.scalar.activation(inter[HIDDEN:P, 0, u * CHUNK:(u + 1) * CHUNK],
                                     x2_ps[u * HIDDEN:(u + 1) * HIDDEN, :], ACT.Copy).then_inc(z3_copied, 1)
            n = 0
            act.wait_ge(products_made, 8 * TILES)
            for hidden, bias, count in ((hidden1, bias1, M1), (hidden2, bias2, M2)):
                for u in range(2):
                    for m in range(count):
                        bank = x1_by_h[:, (n // 2) % 2, (n % 2) * CHUNK:(n % 2 + 1) * CHUNK]
                        act.wait_ge(mlp_made, n + 1)
                        nc.scalar.activation(hidden[:, m, u * CHUNK:(u + 1) * CHUNK], bank, ACT.Relu,
                                             bias=bias[:, m:m + 1]).then_inc(mlp_copied, 1)
                        n += 1
            for u in range(2):
                bank = x1_by_h[:, (n // 2) % 2, (n % 2) * CHUNK:(n % 2 + 1) * CHUNK]
                act.wait_ge(mlp_made, n + 1)
                nc.scalar.activation(y_row[:, u * CHUNK:(u + 1) * CHUNK], bank[0:1, :],
                                     ACT.Copy).then_inc(mlp_copied, 1)
                n += 1


def constants():
    identity = np.eye(P, dtype=np.float32)
    select_h = np.zeros((2, HIDDEN, NJ, HB, FB), np.float32)
    for j in range(NJ):
        for h in range(HB):
            select_h[:, HB * j + h, j, h, :] = 1.0
    same_sample = np.repeat(np.eye(GROUP, dtype=np.float32), DIM, axis=0)
    return identity, select_h.reshape(P, NJ, P), same_sample


def kernel(**inputs):
    import concourse.bacc as bacc
    from concourse.bass_utils import run_bass_kernel_spmd

    x = {k: np.asarray(v) for k, v in inputs.items()}
    identity, select_h, same_sample = constants()
    w0 = x["L0_rec_W0"].reshape(FEATURES, FEATURES, HIDDEN)
    w0_rows = np.stack([np.roll(w0, -FB * i, axis=1)[FB * i:FB * i + FB, 0:HB] for i in range(NI)])
    w0_back = np.stack([np.roll(w0, -FB * i, axis=0)[0:HB, FB * i:FB * i + FB] for i in range(NI)])
    w0_back[:, 0:FB] = 0.0
    arrays = {
        "ids": x["ids"].reshape(TILES, P, FEATURES),
        "w0": w0_rows.transpose(2, 1, 0, 3).reshape(P, NI, HIDDEN),
        "w0_mirror": w0_back.transpose(1, 2, 0, 3).reshape(P, NI, HIDDEN),
        "w1": x["L0_rec_W1"].reshape(NI, FB, NJ, HB, HIDDEN).transpose(3, 1, 2, 0, 4).reshape(P, NJ, NI, HIDDEN),
        "w2": x["L0_rec_W2"].reshape(2, HALF_F, HIDDEN, HIDDEN).transpose(0, 2, 1, 3).reshape(P, HALF_F, HIDDEN),
        "top1": x["W_top1"], "top1_bias": x["b_top1"].reshape(M1, P).T,
        "top2": x["W_top2"], "top2_bias": x["b_top2"].reshape(M2, P).T,
        "top3": x["W_top3"].reshape(M2, P).T, "dense_t": x["dense_ctx"].T,
        "identity": identity, "select_h": select_h, "same_sample": same_sample,
    }
    names = [f"tbl_{f}" for f in range(FEATURES)]
    arrays.update({n: x[n] for n in names})
    arrays = {f"in_{k}": np.ascontiguousarray(v) for k, v in arrays.items()}

    nc = bacc.Bacc("TRN2", target_bir_lowering=False, num_devices=1)
    aps = {k[3:]: nc.dram_tensor(k, v.shape, mybir.dt.from_np(v.dtype), kind="ExternalInput").ap()
           for k, v in arrays.items()}
    out = nc.dram_tensor("out_y", (BATCH, 1), F32, kind="ExternalOutput").ap()
    dlrm_cin_tower(nc, aps["ids"], [aps[n] for n in names], aps["w0"], aps["w0_mirror"], aps["w1"],
                   aps["w2"], aps["top1"], aps["top1_bias"], aps["top2"], aps["top2_bias"], aps["top3"],
                   aps["dense_t"], aps["identity"], aps["select_h"], aps["same_sample"], out)
    result = run_bass_kernel_spmd(nc, [arrays], core_ids=[0])
    return result.results[0]["out_y"]
```

```python
from contextlib import ExitStack

import numpy as np

import concourse.bass as bass
from concourse import mybir

F32 = mybir.dt.float32
F32R = mybir.dt.float32r
I32 = mybir.dt.int32
ALU = mybir.AluOpType
ACT = mybir.ActivationFunctionType

P = 128
BATCH, FEATURES, DIM, HIDDEN = 1024, 24, 16, 64
TILES = BATCH // P
CHUNK = 512
PAIR = 2 * CHUNK
COLUMNS = DIM * P
FB, HB = 8, 16
NI, NJ = FEATURES // FB, HIDDEN // HB
RING = 4
GROUP = P // DIM
GROUPS = P // GROUP
BATCHES = 4
PER_BATCH = GROUPS // BATCHES
HALF_F = FEATURES // 2
BLOCK = (HALF_F + 1) * GROUP
HALF = TILES // 2
TOP1, TOP2 = 512, 256
N_DENSE = 16
M1, M2 = TOP1 // P, TOP2 // P


def dlrm_cin_tower(nc, ids, tables, w0, w0_mirror, w1, w2, top1, top1_bias, top2, top2_bias, top3,
                   dense_t, identity, select_h, same_sample, out):
    with ExitStack() as ctx:
        def sb(name, shape, dtype=F32):
            return ctx.enter_context(nc.sbuf_tensor(name, shape, dtype))

        def ps(name, shape):
            return ctx.enter_context(nc.psum_tensor(name, shape, F32))

        def sem(name):
            return ctx.enter_context(nc.semaphore(name))

        x0_rows = nc.dram_tensor("x0_rows", [TILES, (FEATURES + FB) * DIM, P], F32, kind="Internal").ap()
        x0_groups = nc.dram_tensor("x0_groups", [TILES, P, DIM, FEATURES], F32, kind="Internal").ap()
        x0_f = x0_rows.rearrange("s (f d) b -> s f (d b)", d=DIM)

        ids_all = sb("ids_all", [P, TILES, FEATURES], I32)
        ids_tile = sb("ids_tile", [P, FEATURES], I32)
        embedded = sb("embedded", [P, FEATURES * DIM])
        x0_t = sb("x0_t", [P, NI, P])
        x0_by_f = sb("x0_by_f", [P, 2, NI, PAIR])
        x0_by_g = sb("x0_by_g", [P, 2, NI, PAIR])
        x1_split = sb("x1_split", [P, 2, PAIR], F32R)
        products = sb("products", [P, RING, NI, PAIR])
        embedded_df = sb("embedded_df", [P, DIM, FEATURES])
        x2 = sb("x2", [HIDDEN, P, DIM])
        grouped_x2 = sb("grouped_x2", [P, GROUPS, HIDDEN])
        grouped_x0 = sb("grouped_x0", [P, GROUPS, FEATURES])
        block_x0 = sb("block_x0", [P, GROUPS, 1 + FEATURES, GROUP])
        inter = sb("inter", [P, HALF_F, CHUNK])
        z23 = sb("z23", [P, BATCH])
        z1_a = sb("z1_a", [P, CHUNK])
        z1 = sb("z1", [P, BATCH])
        z1_dense = sb("z1_dense", [HIDDEN + N_DENSE, BATCH])
        upper = sb("upper", [HIDDEN, CHUNK])
        w0_sb = sb("w0_sb", [P, NI, HIDDEN])
        w1_sb = sb("w1_sb", [P, NJ, NI, HIDDEN])
        w2_sb = sb("w2_sb", [P, HALF_F, HIDDEN])
        top1_z1_dense = sb("top1_z1_dense", [HIDDEN + N_DENSE, TOP1])
        top1_z23 = sb("top1_z23", [P, TOP1])
        top2_sb = sb("top2_sb", [P, M1, TOP2])
        top3_sb = sb("top3_sb", [P, M2])
        bias1 = sb("bias1", [P, M1])
        bias2 = sb("bias2", [P, M2])
        ident = sb("ident", [P, P])
        select = sb("select", [P, NJ, P], F32R)
        sample_mask = sb("sample_mask", [P, GROUP])
        hidden1 = sb("hidden1", [P, M1, CHUNK])
        hidden2 = sb("hidden2", [P, M2, CHUNK])

        x1_by_h = ps("x1_by_h", [P, 2, PAIR])
        x1_ps = ps("x1_ps", [P, CHUNK])
        x2_ps = ps("x2_ps", [P, CHUNK])
        group_ps = ps("group_ps", [P, 2, CHUNK])

        select_f32 = hidden1[:, 0, :].rearrange("p (j q) -> p j q", j=NJ)
        w0_mirror_sb = hidden2[:, 0, 0:NI * HIDDEN].rearrange("p (i o) -> p i o", i=NI)
        y_row = hidden1[0:1, 0, :]

        ids_loaded = sem("ids_loaded")
        loaded = sem("loaded")
        ids_ready = sem("ids_ready")
        gathered = [sem(f"gathered_{i}") for i in range(NI)]
        x0_transposed = sem("x0_transposed")
        x0_t_copied = sem("x0_t_copied")
        x0_permuted = sem("x0_permuted")
        x0_stored = sem("x0_stored")
        by_f_loaded = [sem("by_f_loaded_0"), sem("by_f_loaded_1")]
        by_g_loaded = [sem("by_g_loaded_0"), sem("by_g_loaded_1")]
        x0_grouped = sem("x0_grouped")
        w0_ready = sem("w0_ready")
        select_ready = sem("select_ready")
        squares_made = sem("squares_made")
        x1_made = sem("x1_made")
        x1_high = sem("x1_high")
        x1_low = sem("x1_low")
        x1_spread = sem("x1_spread")
        products_made = sem("products_made")
        products_used = sem("products_used")
        x2_copied = sem("x2_copied")
        block_ready = sem("block_ready")
        z1_step = sem("z1_step")
        step_made = sem("step_made")
        step_copied = sem("step_copied")
        z1_moved, z1_added = sem("z1_moved"), sem("z1_added")
        z3_moved, z3_added = sem("z3_moved"), sem("z3_added")
        stored = sem("stored")
        pe_passed, pool_passed = sem("pe_passed"), sem("pool_passed")

        USUAL = (("T0", "T1"), ("T2", "T3"), ("I0",), ("I1",), ("I2",), ("I3",))
        PLANS = {5: (("T0", "T1"), ("T2", "T3", "Z"), ("I0",), ("I1", "A0"), ("A1", "I2"), ("A2", "I3")),
                 6: (("T0", "T1", "A3"), ("T2", "T3"), ("B0", "I0"), ("I1",), ("B1", "I2"), ("I3", "Y")),
                 7: (("T0", "T1"), ("T2", "T3"), ("I0",), ("I1", "I2"), ("I3",), ()),
                 8: (("T0", "T1", "T2", "T3", "I0", "I1", "I2", "I3",
                      "Z", "A0", "A1", "A2", "A3", "B0", "B1", "Y"),)}
        STEP = {}
        for t in sorted(PLANS):
            for name in (name for place in PLANS[t] for name in place):
                STEP[t, name] = 2 * BATCHES * (min(PLANS) - 1) + len(STEP)

        def step_number(t, name):
            if (isinstance(t, int) and t in PLANS):
                return STEP[t, name]
            return 2 * BATCHES * (t - 1) + int(name[1]) + (BATCHES if name[0] == "I" else 0)

        def step_bank(t, name):
            number = step_number(t, name) if isinstance(t, int) else int(name[1])
            return group_ps[:, number % 2, :]

        def steps_at(t, place):
            if isinstance(t, int) and t in PLANS:
                return PLANS[t][place]
            return () if isinstance(t, int) and t == 0 else USUAL[place]

        LOADED = 16 * 15
        block = ctx.enter_context(nc.Block())

        @block.sync
        def _(sp):
            sp.dma_start(ids_all[:], ids.rearrange("s p f -> p s f")).then_inc(ids_loaded, 16)
            for dst, src in (
                (ident[:], identity), (w0_sb[:], w0), (w0_mirror_sb, w0_mirror),
                (select_f32, select_h), (w1_sb[:], w1), (sample_mask[:], same_sample),
                (w2_sb[:], w2), (top1_z1_dense[0:HIDDEN, :], top1[0:HIDDEN, :]),
                (top1_z23[:], top1[HIDDEN:3 * HIDDEN, :]),
                (top1_z1_dense[HIDDEN:, :], top1[3 * HIDDEN:, :]),
                (top2_sb[:], top2.rearrange("(k p) n -> p k n", p=P)), (top3_sb[:], top3),
                (bias1[:], top1_bias), (bias2[:], top2_bias), (z1_dense[HIDDEN:, :], dense_t),
            ):
                sp.dma_start(dst, src).then_inc(loaded, 16)

            def load_by_f(s, c, i):
                sp.dma_start(x0_by_f[:, c, i, :],
                             x0_f[s, FB * i:FB * i + FB, c * PAIR:(c + 1) * PAIR].unsqueeze(0)
                             .broadcast_to([HB, FB, PAIR])).then_inc(by_f_loaded[c], 16)

            def load_by_g(s, c, i):
                sp.dma_start(x0_by_g[:, c, i, :],
                             x0_f[s, FB * i:FB * i + HB, c * PAIR:(c + 1) * PAIR].unsqueeze(1)
                             .broadcast_to([HB, FB, PAIR])).then_inc(by_g_loaded[c], 16)

            for i in range(NI):
                sp.wait_ge(x0_t_copied, i + 1)
                sp.dma_start(x0_rows[0, i * P:(i + 1) * P, :], x0_t[:, i, :]).then_inc(x0_stored, 16)
                if i == 0:
                    sp.dma_start(x0_rows[0, FEATURES * DIM:, :], x0_t[:, 0, :]).then_inc(x0_stored, 16)
                sp.wait_ge(x0_stored, 32 + 16 * i)
                load_by_f(0, 0, i)
                if i >= 1:
                    load_by_g(0, 0, i - 1)
            load_by_g(0, 0, NI - 1)
            for i in range(NI):
                load_by_f(0, 1, i)
                load_by_g(0, 1, i)
            sp.wait_ge(x0_permuted, 1)
            sp.dma_start(x0_groups[0], embedded_df[:]).then_inc(x0_stored, 16)

            with sp.Fori(1, TILES) as s:
                sp.wait_ge(x0_t_copied, s + NI)
                sp.dma_start(x0_rows[s, 0:FEATURES * DIM, :].rearrange("(i p) b -> p i b", p=P),
                             x0_t[:]).then_inc(x0_stored, 16)
                sp.dma_start(x0_rows[s, FEATURES * DIM:, :], x0_t[:, 0, :]).then_inc(x0_stored, 16)
                sp.wait_ge(x0_permuted, s + 1)
                sp.dma_start(x0_groups[s], embedded_df[:]).then_inc(x0_stored, 16)
                sp.wait_ge(x0_stored, 48 * s + 80)
                for c in range(2):
                    sp.wait_ge(x1_made, 2 * s - 1 + c)
                    for i in range(NI):
                        load_by_g(s, c, i)
                    sp.wait_ge(products_made, 8 * s - 4 + 4 * c)
                    for i in range(NI):
                        load_by_f(s, c, i)

        @block.gpsimd
        def _(pool):
            def copy_ids(s):
                nc.gpsimd.tensor_copy(ids_tile[:], ids_all[:, s, :]).then_inc(ids_ready, 1)
                pool.wait_ge(ids_ready, s + 1)
                pool.sem_inc(pool_passed, 1)

            def gather(features):
                for f in features:
                    nc.gpsimd.indirect_dma_start(
                        out=embedded[:, f * DIM:(f + 1) * DIM], out_offset=None, in_=tables[f],
                        in_offset=bass.IndirectOffsetOnAxis(ap=ids_tile[:, f:f + 1], axis=0),
                    ).then_inc(gathered[f // FB], 16)

            def sum_d(s, c):
                part = x1_split[:, c, :].bitcast(F32)
                total = z1[:, bass.ts(s, P)]
                pool.wait_ge(x1_high, 4 * s + 2 * c + 2)
                pool.wait_ge(x1_low, 4 * s + 2 * c + 2)
                done = 7 * s + 3 * c
                if not (isinstance(s, int) and s + c == 0):
                    pool.wait_ge(z1_step, done)
                nc.gpsimd.tensor_tensor(z1_a[:], part[:, 0:CHUNK], part[:, CHUNK:PAIR],
                                        ALU.add).then_inc(z1_step, 1)
                pool.wait_ge(z1_step, done + 1)
                nc.gpsimd.tensor_tensor(z1_a[:, 0:2 * P], z1_a[:, 0:2 * P], z1_a[:, 2 * P:4 * P],
                                        ALU.add).then_inc(z1_step, 1)
                pool.wait_ge(z1_step, done + 2)
                if c == 0:
                    nc.gpsimd.tensor_tensor(total, z1_a[:, 0:P], z1_a[:, P:2 * P],
                                            ALU.add).then_inc(z1_step, 1)
                else:
                    nc.gpsimd.tensor_tensor(z1_a[:, 0:P], z1_a[:, 0:P], z1_a[:, P:2 * P],
                                            ALU.add).then_inc(z1_step, 1)
                    pool.wait_ge(z1_step, done + 3)
                    nc.gpsimd.tensor_tensor(total, total, z1_a[:, 0:P], ALU.add).then_inc(z1_step, 1)

            half = FEATURES // 2
            pool.wait_ge(ids_loaded, 16)
            copy_ids(0)
            gather(range(FEATURES))
            pool.wait_ge(x0_transposed, NI)
            pool.wait_ge(x0_permuted, 1)
            copy_ids(1)
            gather(range(FEATURES))
            sum_d(0, 0)
            with pool.Fori(1, TILES - 1) as s:
                pool.wait_ge(x0_transposed, s + NI)
                pool.wait_ge(x0_permuted, s + 1)
                copy_ids(s + 1)
                gather(range(half))
                sum_d(s - 1, 1)
                gather(range(half, FEATURES))
                sum_d(s, 0)
            sum_d(TILES - 2, 1)
            sum_d(TILES - 1, 0)
            sum_d(TILES - 1, 1)

        @block.tensor
        def _(pe):
            def transpose_x0(s):
                for i in range(NI):
                    pe.wait_ge(gathered[i], 16 * FB * s + 16 * FB)
                    mm = nc.tensor.transpose(x1_ps[:, i * P:(i + 1) * P], embedded[:, i * P:(i + 1) * P], ident[:])
                mm.then_inc(x0_transposed, 1)

            def layer1(s, c):
                pe.wait_ge(squares_made, 2 * s + c + 1)
                for i in range(NI):
                    for u in range(2):
                        mm = nc.tensor.matmul(x1_ps[u * HIDDEN:(u + 1) * HIDDEN, :], w0_sb[:, i, :],
                                              x0_by_g[:, c, i, u * CHUNK:(u + 1) * CHUNK],
                                              start=(i == 0), stop=(i == NI - 1))
                mm.then_inc(x1_made, 1)

            def spread_x1(s, c, j):
                n = 8 * s + 4 * c + j
                if not (isinstance(s, int) and n < 2):
                    pe.wait_ge(products_made, n - 1)
                if j == 0:
                    pe.wait_ge(x1_high, 4 * s + 2 * c + 2)
                    pe.wait_ge(x1_low, 4 * s + 2 * c + 2)
                for u in range(2):
                    cols = slice(u * CHUNK, (u + 1) * CHUNK)
                    mm = nc.tensor.matmul(x1_by_h[:, j % 2, cols], select[:, j, :], x1_split[:, c, cols],
                                          start=True, stop=True)
                mm.then_inc(x1_spread, 1)

            def layer2(s, c, j):
                pe.wait_ge(products_made, 8 * s + 4 * c + j + 1)
                if j == 0 and not (isinstance(s, int) and 2 * s + c == 0):
                    pe.wait_ge(x2_copied, 4 * s + 2 * c)
                for i in range(NI):
                    for u in range(2):
                        mm = nc.tensor.matmul(x2_ps[u * HIDDEN:(u + 1) * HIDDEN, :], w1_sb[:, j, i, :],
                                              products[:, j % RING, i, u * CHUNK:(u + 1) * CHUNK],
                                              start=(j == 0 and i == 0), stop=(j == NJ - 1 and i == NI - 1))
                mm.then_inc(products_used, 1)

            def transpose_groups(bank, s, k):
                if k == 0:
                    pe.wait_ge(x2_copied, 4 * s + 4)
                pe.sem_inc(pe_passed, 1)
                columns = x2[:].rearrange("r (g b) d -> r g (b d)", b=GROUP)
                for n in range(PER_BATCH):
                    mm = nc.tensor.transpose(bank[:, n * HIDDEN:(n + 1) * HIDDEN],
                                             columns[:, k * PER_BATCH + n, :], ident[0:HIDDEN, 0:HIDDEN])
                return mm

            def interact_groups(bank, s, k):
                pe.wait_ge(block_ready, 8 * s + 9)
                for n in range(PER_BATCH):
                    g = k * PER_BATCH + n
                    nc.tensor.matmul(bank[0:HIDDEN, n * BLOCK:(n + 1) * BLOCK],
                                     grouped_x2[:, g, :], block_x0[:, g, 0:1 + HALF_F, :],
                                     start=True, stop=True)
                    mm = nc.tensor.matmul(bank[HIDDEN:P, n * BLOCK + GROUP:(n + 1) * BLOCK],
                                          grouped_x2[:, g, :], block_x0[:, g, 1 + HALF_F:, :],
                                          start=True, stop=True)
                return mm

            def sum_z3(bank, u):
                pe.wait_ge(step_copied, STEP[5 if u == 0 else 8, "Z"] + (1 if u == 0 else 2))
                for t in range(HALF_F):
                    half = t % 2
                    mm = nc.tensor.matmul(bank[half * HIDDEN:(half + 1) * HIDDEN, :], w2_sb[:, t, :],
                                          inter[:, t, :], start=(t < 2), stop=(t >= HALF_F - 2))
                return mm

            def mlp1(bank, u, m):
                cols, units = slice(u * CHUNK, (u + 1) * CHUNK), slice(m * P, (m + 1) * P)
                pe.wait_ge(z1_added, u + 1)
                nc.tensor.matmul(bank, top1_z1_dense[:, units], z1_dense[:, cols], start=True, stop=False)
                pe.wait_ge(z3_added, u + 1)
                return nc.tensor.matmul(bank, top1_z23[:, units], z23[:, cols], start=False, stop=True)

            def mlp2(bank, t, m):
                pe.wait_ge(step_copied, STEP[t, "A3"] + 3)
                for k in range(M1):
                    mm = nc.tensor.matmul(bank, top2_sb[:, k, m * P:(m + 1) * P], hidden1[:, k, :],
                                          start=(k == 0), stop=(k == M1 - 1))
                return mm

            def mlp3(bank, t):
                pe.wait_ge(step_copied, STEP[t, "B1"] + 3)
                for k in range(M2):
                    mm = nc.tensor.matmul(bank[0:1, :], top3_sb[:, k:k + 1], hidden2[:, k, :],
                                          start=(k == 0), stop=(k == M2 - 1))
                return mm

            def steps(t, place):
                for name in steps_at(t, place):
                    number, bank = step_number(t, name), step_bank(t, name)
                    pe.wait_ge(step_copied, number + 1)
                    if isinstance(t, int) and (t, "Z") in STEP and number == STEP[t, "Z"] + 2:
                        pe.wait_ge(z3_added, 1 if t == 5 else 2)
                    u, m = (1 if isinstance(t, int) and t == 8 else 0), int(name[1:] or 0)
                    if name[0] == "T":
                        mm = transpose_groups(bank, t - 1, m)
                    elif name[0] == "I":
                        mm = interact_groups(bank, t - 1, m)
                    elif name == "Z":
                        mm = sum_z3(bank, u)
                    elif name[0] == "A":
                        mm = mlp1(bank, u, m)
                    elif name[0] == "B":
                        mm = mlp2(bank, 8 if t == 8 else 6, m)
                    else:
                        mm = mlp3(bank, t)
                    mm.then_inc(step_made, 1)

            def tile(s, last=False):
                if not last:
                    transpose_x0(s + 1)
                layer2(s, 0, 0)
                spread_x1(s, 0, 3)
                if not last:
                    pe.wait_ge(x0_t_copied, s + 1 + NI)
                layer1(s, 1)
                steps(s, 0)
                layer2(s, 0, 1)
                steps(s, 1)
                spread_x1(s, 1, 0)
                layer2(s, 0, 2)
                spread_x1(s, 1, 1)
                layer2(s, 0, 3)
                spread_x1(s, 1, 2)
                steps(s, 2)
                layer2(s, 1, 0)
                spread_x1(s, 1, 3)
                if not last:
                    layer1(s + 1, 0)
                steps(s, 3)
                layer2(s, 1, 1)
                steps(s, 4)
                if not last:
                    spread_x1(s + 1, 0, 0)
                layer2(s, 1, 2)
                if not last:
                    spread_x1(s + 1, 0, 1)
                layer2(s, 1, 3)
                if not last:
                    spread_x1(s + 1, 0, 2)
                steps(s, 5)

            pe.wait_ge(loaded, LOADED)
            for i, bank in enumerate((x1_ps, x2_ps, group_ps[:, 0, :])):
                pe.wait_ge(gathered[i], 16 * FB)
                nc.tensor.transpose(bank[:, 0:P], embedded[:, i * P:(i + 1) * P], ident[:]
                                    ).then_inc(x0_transposed, 1)
            pe.wait_ge(w0_ready, 1)
            pe.wait_ge(select_ready, 1)
            pe.wait_ge(x0_t_copied, NI)
            layer1(0, 0)
            for j in range(NJ - 1):
                spread_x1(0, 0, j)
            tile(0)
            with pe.Fori(1, HALF + 1) as s:
                tile(s)
            tile(5)
            tile(6)
            tile(7, last=True)
            steps(8, 0)

        @block.vector
        def _(dve):
            def square(s, c):
                dve.wait_ge(by_f_loaded[c], 48 * s + 48)
                dve.wait_ge(by_g_loaded[c], 48 * s + 48)
                nc.vector.tensor_tensor(x0_by_g[:, c], x0_by_f[:, c], x0_by_g[:, c],
                                        ALU.mult).then_inc(squares_made, 1)

            def product(s, c, j):
                n = 8 * s + 4 * c + j
                dve.wait_ge(x1_spread, n + 1)
                if not (isinstance(s, int) and n < RING):
                    dve.wait_ge(products_used, n + 1 - RING)
                spread = x1_by_h[:, j % 2, :].unsqueeze(1).broadcast_to([P, NI, PAIR])
                nc.vector.tensor_tensor(products[:, j % RING], x0_by_f[:, c], spread,
                                        ALU.mult).then_inc(products_made, 1)

            def low_part(s, c):
                dve.wait_ge(x1_high, 4 * s + 2 * c + 2)
                for u in range(2):
                    here, there = slice(u * HIDDEN, (u + 1) * HIDDEN), slice((1 - u) * HIDDEN, (2 - u) * HIDDEN)
                    cols = slice(u * CHUNK, (u + 1) * CHUNK)
                    nc.vector.tensor_tensor(x1_split[there, c, cols], x1_ps[here, :], x1_split[here, c, cols],
                                            ALU.subtract).then_inc(x1_low, 1)

            def add_z1(u):
                cols = slice(u * CHUNK, (u + 1) * CHUNK)
                dve.wait_ge(z1_moved, u + 1)
                nc.vector.tensor_tensor(z1_dense[0:HIDDEN, cols], z1[0:HIDDEN, cols], upper[:],
                                        ALU.add).then_inc(z1_added, 1)

            def add_z3(u):
                bank = step_bank(8 if u else 5, "Z")
                dve.wait_ge(z3_moved, u + 1)
                nc.vector.tensor_tensor(z23[HIDDEN:P, u * CHUNK:(u + 1) * CHUNK], bank[0:HIDDEN, :], upper[:],
                                        ALU.add).then_inc(z3_added, 1)

            def pair(s, c, nxt, mlp=False):
                product(s, c, 0)
                if mlp:
                    add_z1(0)
                product(s, c, 1)
                if nxt is not None:
                    square(*nxt)
                product(s, c, 2)
                if nxt is not None:
                    low_part(*nxt)
                product(s, c, 3)
                if mlp:
                    add_z3(0)

            dve.wait_ge(loaded, LOADED)
            nc.vector.tensor_tensor(w0_sb[HIDDEN:P], w0_sb[HIDDEN:P], w0_mirror_sb[HIDDEN:P],
                                    ALU.add).then_inc(w0_ready, 1)
            nc.vector.tensor_copy(select[:], select_f32).then_inc(select_ready, 1)
            square(0, 0)
            low_part(0, 0)
            pair(0, 0, (0, 1))
            pair(0, 1, (1, 0))
            with dve.Fori(1, HALF + 1) as s:
                pair(s, 0, (s, 1))
                pair(s, 1, (s + 1, 0))
            pair(5, 0, (5, 1), mlp=True)
            pair(5, 1, (6, 0))
            pair(6, 0, (6, 1))
            pair(6, 1, (7, 0))
            pair(7, 0, (7, 1))
            pair(7, 1, None)
            add_z1(1)
            add_z3(1)

        @block.scalar
        def _(act):
            def copy_x0(s):
                for i in range(NI):
                    act.wait_ge(gathered[i], 16 * FB * s + 16 * FB)
                act.wait_ge(x0_stored, 48 * s + 32)
                nc.scalar.activation(embedded_df[:], embedded[:].rearrange("p (f d) -> p d f", d=DIM),
                                     ACT.Copy).then_inc(x0_permuted, 1)
                act.wait_ge(x0_transposed, s + NI)
                nc.scalar.activation(x0_t[:], x1_ps[:, 0:NI * P].rearrange("p (i b) -> p i b", i=NI),
                                     ACT.Copy).then_inc(x0_t_copied, 1)

            def high_part(s, c):
                act.wait_ge(x1_made, 2 * s + c + 1)
                if not (isinstance(s, int) and s == 0):
                    act.wait_ge(z1_step, 7 * s - 4 + 4 * c)
                    act.wait_ge(x1_spread, 8 * s - 4 + 4 * c)
                for u in range(2):
                    rows, cols = slice(u * HIDDEN, (u + 1) * HIDDEN), slice(u * CHUNK, (u + 1) * CHUNK)
                    nc.scalar.activation(x1_split[rows, c, cols], x1_ps[rows, :],
                                         ACT.Copy).then_inc(x1_high, 1)

            def copy_x2(s, c):
                act.wait_ge(products_used, 8 * s + 4 * c + 4)
                if c == 0 and not (isinstance(s, int) and s == 0):
                    act.wait_ge(step_made, step_number(s, "T3") + 1)
                for u in range(2):
                    d0, dims = 8 * c + 4 * u, CHUNK // P
                    nc.scalar.activation(x2[:, :, d0:d0 + dims].rearrange("r b d -> r d b"),
                                         x2_ps[u * HIDDEN:(u + 1) * HIDDEN, :].rearrange("r (d b) -> r d b", d=dims),
                                         ACT.Copy).then_inc(x2_copied, 1)

            def block_diagonal(s):
                act.wait_ge(x0_grouped, 16 * s + 16)
                for b in range(GROUP):
                    nc.scalar.activation(block_x0[:, :, 1:, b], grouped_x0[:], ACT.Copy,
                                         scale=sample_mask[:, b:b + 1]).then_inc(block_ready, 1)

            def load_groups(s, first=False):
                act.wait_ge(x0_stored, 48 * s + 80)
                if not first:
                    act.wait_ge(block_ready, 8 * s + 1)
                act.dma_start(grouped_x0[:], x0_groups[s].rearrange("(g b) d f -> (b d) g f", b=GROUP)
                              ).then_inc(x0_grouped, 16)

            def copy_groups(bank, s, k):
                return nc.scalar.activation(grouped_x2[:, k * PER_BATCH:(k + 1) * PER_BATCH, :],
                                            bank[:, 0:PER_BATCH * HIDDEN].rearrange(
                                                "p (n r) -> p n r", n=PER_BATCH), ACT.Copy)

            def copy_interactions(bank, s, k):
                first = k * PER_BATCH * GROUP
                in_half = s % HALF if isinstance(s, int) else s
                block = bank[:, 0:PER_BATCH * BLOCK].rearrange("p (n t b) -> p t n b", n=PER_BATCH, b=GROUP)
                nc.scalar.activation(
                    z23[0:HIDDEN, bass.ds(s * P + first, PER_BATCH * GROUP)].rearrange(
                        "p (n b) -> p n b", n=PER_BATCH), block[0:HIDDEN, 0], ACT.Copy)
                return nc.scalar.activation(
                    inter[:, :, bass.ds(in_half * P + first, PER_BATCH * GROUP)].rearrange(
                        "p t (n b) -> p t n b", n=PER_BATCH), block[:, 1:], ACT.Copy)

            def move_z1(u):
                act.wait_ge(z1_step, 7 * HALF * (u + 1))
                nc.scalar.activation(upper[:], z1[HIDDEN:P, u * CHUNK:(u + 1) * CHUNK],
                                     ACT.Copy).then_inc(z1_moved, 1)

            def move_z3(bank, u):
                act.wait_ge(z1_added, u + 1)
                act_moved = nc.scalar.activation(upper[:], bank[HIDDEN:P, :], ACT.Copy)
                act_moved.then_inc(z3_moved, 1)
                act.wait_ge(z3_moved, u + 1)
                return act.sem_inc(step_copied, 1)

            def relu(to, bank, bias, m):
                return nc.scalar.activation(to[:, m, :], bank, ACT.Relu, bias=bias[:, m:m + 1])

            def copies(t, place):
                for name in steps_at(t, place):
                    number, bank = step_number(t, name), step_bank(t, name)
                    act.wait_ge(step_made, number + 1)
                    u, m = (1 if isinstance(t, int) and t == 8 else 0), int(name[1:] or 0)
                    if name[0] == "T":
                        copy_groups(bank, t - 1, m).then_inc(step_copied, 1)
                    elif name[0] == "I":
                        copy_interactions(bank, t - 1, m).then_inc(step_copied, 1)
                    elif name == "Z":
                        move_z3(bank, u)
                    elif name[0] == "A":
                        relu(hidden1, bank, bias1, m).then_inc(step_copied, 1)
                    elif name[0] == "B":
                        relu(hidden2, bank, bias2, m).then_inc(step_copied, 1)
                    else:
                        nc.scalar.activation(y_row, bank[0:1, :], ACT.Copy).then_inc(step_copied, 1)
                        act.wait_ge(step_copied, number + 3)
                        act.dma_start(out.rearrange("b o -> o b")[:, u * CHUNK:(u + 1) * CHUNK], y_row
                                      ).then_inc(stored, 16)

            def tile(s, first=False, last=False):
                if not last:
                    copy_x0(s + 1)
                if isinstance(s, int) and s == 5:
                    move_z1(0)
                high_part(s, 1)
                copies(s, 0)
                copies(s, 1)
                if not first:
                    block_diagonal(s - 1)
                copy_x2(s, 0)
                copies(s, 2)
                load_groups(s, first)
                if not last:
                    high_part(s + 1, 0)
                copies(s, 3)
                copies(s, 4)
                if last:
                    block_diagonal(s)
                    move_z1(1)
                copy_x2(s, 1)
                copies(s, 5)

            act.wait_ge(loaded, LOADED)
            act.sem_inc(step_copied, 2)
            nc.scalar.activation(block_x0[:, :, 0, :], sample_mask[:].unsqueeze(1).broadcast_to([P, GROUPS, GROUP]),
                                 ACT.Copy).then_inc(block_ready, 1)
            for i, bank in enumerate((x1_ps, x2_ps, group_ps[:, 0, :])):
                act.wait_ge(x0_transposed, i + 1)
                nc.scalar.activation(x0_t[:, i, :], bank[:, 0:P], ACT.Copy).then_inc(x0_t_copied, 1)
            nc.scalar.activation(embedded_df[:], embedded[:].rearrange("p (f d) -> p d f", d=DIM),
                                 ACT.Copy).then_inc(x0_permuted, 1)
            high_part(0, 0)
            tile(0, first=True)
            with act.Fori(1, HALF + 1) as s:
                tile(s)
            tile(5)
            tile(6)
            tile(7, last=True)
            copies(8, 0)
            act.wait_ge(stored, 32)


def constants():
    identity = np.eye(P, dtype=np.float32)
    select_h = np.zeros((2, HIDDEN, NJ, HB, FB), np.float32)
    for j in range(NJ):
        for h in range(HB):
            select_h[:, HB * j + h, j, h, :] = 1.0
    same_sample = np.repeat(np.eye(GROUP, dtype=np.float32), DIM, axis=0)
    return identity, select_h.reshape(P, NJ, P), same_sample


def kernel(**inputs):
    import concourse.bacc as bacc
    from concourse.bass_utils import run_bass_kernel_spmd

    x = {k: np.asarray(v) for k, v in inputs.items()}
    identity, select_h, same_sample = constants()
    w0 = x["L0_rec_W0"].reshape(FEATURES, FEATURES, HIDDEN)
    w0_rows = np.stack([np.roll(w0, -FB * i, axis=1)[FB * i:FB * i + FB, 0:HB] for i in range(NI)])
    w0_back = np.stack([np.roll(w0, -FB * i, axis=0)[0:HB, FB * i:FB * i + FB] for i in range(NI)])
    w0_back[:, 0:FB] = 0.0
    arrays = {
        "ids": x["ids"].reshape(TILES, P, FEATURES),
        "w0": w0_rows.transpose(2, 1, 0, 3).reshape(P, NI, HIDDEN),
        "w0_mirror": w0_back.transpose(1, 2, 0, 3).reshape(P, NI, HIDDEN),
        "w1": x["L0_rec_W1"].reshape(NI, FB, NJ, HB, HIDDEN).transpose(3, 1, 2, 0, 4).reshape(P, NJ, NI, HIDDEN),
        "w2": x["L0_rec_W2"].reshape(2, HALF_F, HIDDEN, HIDDEN).transpose(0, 2, 1, 3).reshape(P, HALF_F, HIDDEN),
        "top1": x["W_top1"], "top1_bias": x["b_top1"].reshape(M1, P).T,
        "top2": x["W_top2"], "top2_bias": x["b_top2"].reshape(M2, P).T,
        "top3": x["W_top3"].reshape(M2, P).T, "dense_t": x["dense_ctx"].T,
        "identity": identity, "select_h": select_h, "same_sample": same_sample,
    }
    names = [f"tbl_{f}" for f in range(FEATURES)]
    arrays.update({n: x[n] for n in names})
    arrays = {f"in_{k}": np.ascontiguousarray(v) for k, v in arrays.items()}

    nc = bacc.Bacc("TRN2", target_bir_lowering=False, num_devices=1)
    aps = {k[3:]: nc.dram_tensor(k, v.shape, mybir.dt.from_np(v.dtype), kind="ExternalInput").ap()
           for k, v in arrays.items()}
    out = nc.dram_tensor("out_y", (BATCH, 1), F32, kind="ExternalOutput").ap()
    dlrm_cin_tower(nc, aps["ids"], [aps[n] for n in names], aps["w0"], aps["w0_mirror"], aps["w1"],
                   aps["w2"], aps["top1"], aps["top1_bias"], aps["top2"], aps["top2_bias"], aps["top3"],
                   aps["dense_t"], aps["identity"], aps["select_h"], aps["same_sample"], out)
    result = run_bass_kernel_spmd(nc, [arrays], core_ids=[0])
    return result.results[0]["out_y"]
```

```python
from contextlib import ExitStack

import numpy as np

import concourse.bass as bass
from concourse import mybir

F32 = mybir.dt.float32
F32R = mybir.dt.float32r
I32 = mybir.dt.int32
ALU = mybir.AluOpType
ACT = mybir.ActivationFunctionType

P = 128
BATCH, FEATURES, DIM, HIDDEN = 1024, 24, 16, 64
TILES = BATCH // P
CHUNK = 512
PAIR = 2 * CHUNK
COLUMNS = DIM * P
FB, HB = 8, 16
NI, NJ = FEATURES // FB, HIDDEN // HB
RING = 4
GROUP = P // DIM
GROUPS = P // GROUP
BATCHES = 4
PER_BATCH = GROUPS // BATCHES
HALF_F = FEATURES // 2
BLOCK = (HALF_F + 1) * GROUP
TOP1, TOP2 = 512, 256
N_DENSE = 16
M1, M2 = TOP1 // P, TOP2 // P


def dlrm_cin_tower(nc, ids, tables, w0, w0_mirror, w1, w2, top1, top1_bias, top2, top2_bias, top3,
                   dense_t, identity, select_h, same_sample, out):
    with ExitStack() as ctx:
        def sb(name, shape, dtype=F32):
            return ctx.enter_context(nc.sbuf_tensor(name, shape, dtype))

        def ps(name, shape):
            return ctx.enter_context(nc.psum_tensor(name, shape, F32))

        def sem(name):
            return ctx.enter_context(nc.semaphore(name))

        x0_rows = nc.dram_tensor("x0_rows", [TILES, (FEATURES + FB) * DIM, P], F32, kind="Internal").ap()
        x0_groups = nc.dram_tensor("x0_groups", [TILES, P, DIM, FEATURES], F32, kind="Internal").ap()
        x0_f = x0_rows.rearrange("s (f d) b -> s f (d b)", d=DIM)

        ids_all = sb("ids_all", [P, TILES, FEATURES], I32)
        ids_tile = sb("ids_tile", [P, 2, FEATURES], I32)
        embedded = sb("embedded", [P, 2, FEATURES * DIM])
        x0_t = sb("x0_t", [P, NI, P])
        x0_by_f = sb("x0_by_f", [P, 2, NI, PAIR])
        x0_by_g = sb("x0_by_g", [P, 2, NI, PAIR])
        x1_split = sb("x1_split", [P, 2, PAIR], F32R)
        products = sb("products", [P, RING, NI, PAIR])
        embedded_df = sb("embedded_df", [P, DIM, FEATURES])
        x2 = sb("x2", [HIDDEN, P, DIM])
        grouped_x2 = sb("grouped_x2", [P, GROUPS, HIDDEN])
        grouped_x0 = sb("grouped_x0", [P, GROUPS, FEATURES])
        block_x0 = sb("block_x0", [P, GROUPS, 1 + FEATURES, GROUP])
        inter = sb("inter", [P, HALF_F, P])
        z23 = sb("z23", [P, BATCH])
        z1_a = sb("z1_a", [P, CHUNK])
        z1 = sb("z1", [P, BATCH])
        z1_dense = sb("z1_dense", [HIDDEN + N_DENSE, BATCH])
        z1_upper = sb("z1_upper", [HIDDEN, P])
        z3_upper = sb("z3_upper", [HIDDEN, P])
        w0_sb = sb("w0_sb", [P, NI, HIDDEN])
        w1_sb = sb("w1_sb", [P, NJ, NI, HIDDEN])
        w2_sb = sb("w2_sb", [P, HALF_F, HIDDEN])
        top1_z1_dense = sb("top1_z1_dense", [HIDDEN + N_DENSE, TOP1])
        top1_z23 = sb("top1_z23", [P, TOP1])
        top2_sb = sb("top2_sb", [P, M1, TOP2])
        top3_sb = sb("top3_sb", [P, M2])
        bias1 = sb("bias1", [P, M1])
        bias2 = sb("bias2", [P, M2])
        ident = sb("ident", [P, P])
        select = sb("select", [P, NJ, P], F32R)
        sample_mask = sb("sample_mask", [P, GROUP])
        hidden1 = sb("hidden1", [P, M1, P])
        hidden2 = sb("hidden2", [P, M2, P])
        y_row = sb("y_row", [1, BATCH])

        x1_by_h = ps("x1_by_h", [P, 2, PAIR])
        x1_ps = ps("x1_ps", [P, CHUNK])
        x2_ps = ps("x2_ps", [P, CHUNK])
        group_ps = ps("group_ps", [P, 2, CHUNK])

        select_f32 = hidden1[:]
        w0_mirror_sb = hidden2[:].rearrange("p m b -> p (m b)")[:, 0:NI * HIDDEN].rearrange("p (i o) -> p i o", i=NI)

        ids_loaded = sem("ids_loaded")
        loaded = sem("loaded")
        ids_ready = sem("ids_ready")
        gathered = [[sem(f"gathered_{parity}_{i}") for i in range(NI)] for parity in range(2)]
        x0_transposed = sem("x0_transposed")
        x0_t_copied = sem("x0_t_copied")
        x0_permuted = sem("x0_permuted")
        x0_stored = sem("x0_stored")
        head_loaded = [sem(f"head_loaded_{i}") for i in range(NI)]
        by_f_loaded = [[sem(f"by_f_loaded_{c}_{i}") for i in range(NI)] for c in range(2)]
        by_g_loaded = [sem("by_g_loaded_0"), sem("by_g_loaded_1")]
        x0_grouped = sem("x0_grouped")
        w0_ready = sem("w0_ready")
        select_ready = sem("select_ready")
        squares_made = sem("squares_made")
        x1_made = sem("x1_made")
        x1_high = sem("x1_high")
        x1_low = sem("x1_low")
        x1_spread = sem("x1_spread")
        products_made = sem("products_made")
        products_used = sem("products_used")
        x2_copied = sem("x2_copied")
        block_ready = sem("block_ready")
        z1_step = sem("z1_step")
        step_made = sem("step_made")
        step_copied = sem("step_copied")
        z1_moved, z1_added = sem("z1_moved"), sem("z1_added")
        z3_moved, z3_added = sem("z3_moved"), sem("z3_added")
        stored = sem("stored")
        pe_passed, pool_passed = sem("pe_passed"), sem("pool_passed")

        PLACES = (("T0", "T1"), ("T2", "T3"), ("I0", "I1"), ("I2", "I3"), ("Z",),
                  ("A0", "A1"), ("A2", "A3"), ("B0", "B1"), ("Y",))
        STEPS = tuple(name for place in PLACES for name in place)
        OFFSET = {name: n for n, name in enumerate(STEPS)}

        LAST = TILES - 1
        END = tuple((LAST - 1 if before else LAST, name) for before, names in (
            (True, "A0 A1 A2 A3"), (False, "T0 T1 T2 T3 I0 I1 I2 I3"), (True, "B0"), (False, "Z"),
            (True, "B1"), (False, "A0 A1 A2 A3"), (True, "Y"), (False, "B0 B1 Y")) for name in names.split())
        END_FIRST = len(STEPS) * (LAST - 1) + OFFSET["A0"]
        END_NUMBER = {step: END_FIRST + n for n, step in enumerate(END)}
        STEPS_MADE = END_FIRST + len(END)
        END_BANKS = [group_ps[:, (END_FIRST + n) % 2, :] for n in range(2)] + [
            x1_by_h[:, j, u * CHUNK:(u + 1) * CHUNK] for j in range(2) for u in range(2)]

        def in_end(s, name):
            return isinstance(s, int) and (s, name) in END_NUMBER

        def step_number(s, name):
            return END_NUMBER[s, name] if in_end(s, name) else len(STEPS) * s + OFFSET[name]

        def step_bank(s, name):
            if in_end(s, name):
                return END_BANKS[(END_NUMBER[s, name] - END_FIRST) % len(END_BANKS)]
            return group_ps[:, OFFSET[name] % 2, :]

        def rows_gathered(s, parity):
            return 8 * FB * (s + 2 - parity)

        def x0_bank(s):
            return group_ps[:, 0, :] if isinstance(s, int) and s == 1 else x1_ps

        LOADED = 16 * 15
        block = ctx.enter_context(nc.Block())

        @block.sync
        def _(sp):
            sp.dma_start(ids_all[:], ids.rearrange("s p f -> p s f")).then_inc(ids_loaded, 16)
            for dst, src in (
                (ident[:], identity), (w0_sb[:], w0), (w0_mirror_sb, w0_mirror),
                (select_f32, select_h), (w1_sb[:], w1), (sample_mask[:], same_sample),
                (w2_sb[:], w2), (top1_z1_dense[0:HIDDEN, :], top1[0:HIDDEN, :]),
                (top1_z23[:], top1[HIDDEN:3 * HIDDEN, :]),
                (top1_z1_dense[HIDDEN:, :], top1[3 * HIDDEN:, :]),
                (top2_sb[:], top2.rearrange("(k p) n -> p k n", p=P)), (top3_sb[:], top3),
                (bias1[:], top1_bias), (bias2[:], top2_bias), (z1_dense[HIDDEN:, :], dense_t),
            ):
                sp.dma_start(dst, src).then_inc(loaded, 16)

            def load_by_f(s, c, i):
                sp.dma_start(x0_by_f[:, c, i, :],
                             x0_f[s, FB * i:FB * i + FB, c * PAIR:(c + 1) * PAIR].unsqueeze(0)
                             .broadcast_to([HB, FB, PAIR])).then_inc(by_f_loaded[c][i], 16)

            def load_by_g(s, c, i):
                sp.dma_start(x0_by_g[:, c, i, :],
                             x0_f[s, FB * i:FB * i + HB, c * PAIR:(c + 1) * PAIR].unsqueeze(1)
                             .broadcast_to([HB, FB, PAIR])).then_inc(by_g_loaded[c], 16)

            def load_head_by_f(i):
                sp.dma_start(x0_by_f[:, 0, i, :],
                             x0_f[0, FB * i:FB * i + FB, 0:PAIR].unsqueeze(0)
                             .broadcast_to([HB, FB, PAIR])).then_inc(head_loaded[i], 16)

            def load_head_by_g(i, half):
                f = FB * ((i + half) % NI)
                sp.dma_start(x0_by_g[half * P // 2:(half + 1) * P // 2, 0, i, :],
                             x0_f[0, f:f + FB, 0:PAIR].unsqueeze(1)
                             .broadcast_to([FB, FB, PAIR])).then_inc(head_loaded[i], 16)

            for i in range(NI):
                sp.wait_ge(x0_t_copied, i + 1)
                sp.dma_start(x0_rows[0, i * P:(i + 1) * P, :], x0_t[:, i, :]).then_inc(x0_stored, 16)
                if i == 0:
                    sp.dma_start(x0_rows[0, FEATURES * DIM:, :], x0_t[:, 0, :]).then_inc(x0_stored, 16)
                sp.wait_ge(x0_stored, 32 + 16 * i)
                load_head_by_g((i - 1) % NI, 1)
                load_head_by_f(i)
                load_head_by_g(i, 0)
            for i in range(NI):
                load_by_f(0, 1, i)
                load_by_g(0, 1, i)
            sp.wait_ge(x0_permuted, 1)
            sp.dma_start(x0_groups[0], embedded_df[:]).then_inc(x0_stored, 16)

            with sp.Fori(1, TILES) as s:
                sp.wait_ge(x0_t_copied, s + NI)
                sp.dma_start(x0_rows[s, 0:FEATURES * DIM, :].rearrange("(i p) b -> p i b", p=P),
                             x0_t[:]).then_inc(x0_stored, 16)
                sp.dma_start(x0_rows[s, FEATURES * DIM:, :], x0_t[:, 0, :]).then_inc(x0_stored, 16)
                sp.wait_ge(x0_permuted, s + 1)
                sp.dma_start(x0_groups[s], embedded_df[:]).then_inc(x0_stored, 16)
                sp.wait_ge(x0_stored, 48 * s + 80)
                for c in range(2):
                    sp.wait_ge(x1_made, 2 * s - 1 + c)
                    for i in range(NI):
                        load_by_g(s, c, i)
                    sp.wait_ge(products_made, 8 * s - 4 + 4 * c)
                    for i in range(NI):
                        load_by_f(s, c, i)

        @block.gpsimd
        def _(pool):
            def copy_ids(s, parity):
                nc.gpsimd.tensor_copy(ids_tile[:, parity], ids_all[:, s, :]).then_inc(ids_ready, 1)
                pool.wait_ge(ids_ready, s + 1)
                pool.sem_inc(pool_passed, 1)

            def gather(parity, features):
                for f in features:
                    nc.gpsimd.indirect_dma_start(
                        out=embedded[:, parity, f * DIM:(f + 1) * DIM], out_offset=None, in_=tables[f],
                        in_offset=bass.IndirectOffsetOnAxis(ap=ids_tile[:, parity, f:f + 1], axis=0),
                    ).then_inc(gathered[parity][f // FB], 16)

            def fold_chunks(s, c):
                part = x1_split[:, c, :].bitcast(F32)
                pool.wait_ge(x1_high, 4 * s + 2 * c + 2)
                pool.wait_ge(x1_low, 4 * s + 2 * c + 2)
                done = 7 * s + 3 * c + 1
                pool.wait_ge(z1_step, done)
                nc.gpsimd.tensor_tensor(z1_a[:], part[:, 0:CHUNK], part[:, CHUNK:PAIR],
                                        ALU.add).then_inc(z1_step, 1)

            def sum_d(s, c):
                done = 7 * s + 3 * c + 1
                total = z1[:, bass.ts(s, P)]
                pool.wait_ge(z1_step, done + 1)
                nc.gpsimd.tensor_tensor(z1_a[:, 0:2 * P], z1_a[:, 0:2 * P], z1_a[:, 2 * P:4 * P],
                                        ALU.add).then_inc(z1_step, 1)
                pool.wait_ge(z1_step, done + 2)
                pool.sem_inc(pool_passed, 1)
                if c == 0:
                    nc.gpsimd.tensor_tensor(total, z1_a[:, 0:P], z1_a[:, P:2 * P],
                                            ALU.add).then_inc(z1_step, 1)
                else:
                    nc.gpsimd.tensor_tensor(z1_a[:, 0:P], z1_a[:, 0:P], z1_a[:, P:2 * P],
                                            ALU.add).then_inc(z1_step, 1)
                    pool.wait_ge(z1_step, done + 3)
                    pool.sem_inc(pool_passed, 1)
                    nc.gpsimd.tensor_tensor(total, total, z1_a[:, 0:P], ALU.add).then_inc(z1_step, 1)

            half = FEATURES // 2
            pool.wait_ge(ids_loaded, 16)
            copy_ids(0, 0)
            gather(0, range(FEATURES))
            copy_ids(1, 1)
            gather(1, range(FEATURES))
            pool.sem_inc(z1_step, 1)

            def tile(s, parity):
                pool.wait_ge(x0_transposed, s - 1 + NI)
                pool.wait_ge(x0_permuted, s)
                copy_ids(s + 1, 1 - parity)
                gather(1 - parity, range(half))
                fold_chunks(s - 1, 0)
                gather(1 - parity, range(half, FEATURES))
                sum_d(s - 1, 0)
                fold_chunks(s - 1, 1)
                sum_d(s - 1, 1)

            with pool.Fori(0, TILES // 2 - 1) as n:
                tile(2 * n + 1, 1)
                tile(2 * n + 2, 0)
            for s in range(TILES - 2, TILES):
                for c in range(2):
                    fold_chunks(s, c)
                    sum_d(s, c)

        @block.tensor
        def _(pe):
            def transpose_x0(s, parity):
                for i in range(NI):
                    pe.wait_ge(gathered[parity][i], rows_gathered(s, parity))
                    mm = nc.tensor.transpose(x0_bank(s)[:, i * P:(i + 1) * P], embedded[:, parity, i * P:(i + 1) * P],
                                             ident[:])
                mm.then_inc(x0_transposed, 1)

            def keep_warm(n):
                for _ in range(n):
                    nc.tensor.matmul(x2_ps[:], ident[:], w1_sb[:].rearrange("p j i o -> p (j i o)")[:, 0:CHUNK],
                                     start=True, stop=True)

            def layer1(s, c):
                for i in range(NI):
                    if isinstance(s, int) and s + c == 0:
                        keep_warm((0, 4, 1)[i])
                    pe.wait_ge(squares_made, 2 * NI * s + NI * c + i + 1)
                    for u in range(2):
                        mm = nc.tensor.matmul(x1_ps[u * HIDDEN:(u + 1) * HIDDEN, :], w0_sb[:, i, :],
                                              x0_by_g[:, c, i, u * CHUNK:(u + 1) * CHUNK],
                                              start=(i == 0), stop=(i == NI - 1))
                mm.then_inc(x1_made, 1)

            def spread_x1(s, c, j):
                n = 8 * s + 4 * c + j
                if not (isinstance(s, int) and n < 2):
                    pe.wait_ge(products_made, n - 1)
                if j == 0:
                    pe.wait_ge(x1_high, 4 * s + 2 * c + 2)
                    pe.wait_ge(x1_low, 4 * s + 2 * c + 2)
                for u in range(2):
                    cols = slice(u * CHUNK, (u + 1) * CHUNK)
                    mm = nc.tensor.matmul(x1_by_h[:, j % 2, cols], select[:, j, :], x1_split[:, c, cols],
                                          start=True, stop=True)
                mm.then_inc(x1_spread, 1)

            def layer2(s, c, j, row_tiles=range(NI)):
                if 0 in row_tiles:
                    pe.wait_ge(products_made, 8 * s + 4 * c + j + 1)
                if j == 0 and not (isinstance(s, int) and 2 * s + c == 0):
                    pe.wait_ge(x2_copied, 4 * s + 2 * c)
                for i in row_tiles:
                    for u in range(2):
                        mm = nc.tensor.matmul(x2_ps[u * HIDDEN:(u + 1) * HIDDEN, :], w1_sb[:, j, i, :],
                                              products[:, j % RING, i, u * CHUNK:(u + 1) * CHUNK],
                                              start=(j == 0 and i == 0), stop=(j == NJ - 1 and i == NI - 1))
                if NI - 1 in row_tiles:
                    mm.then_inc(products_used, 1)

            def transpose_groups(bank, s, k):
                if k == 0:
                    pe.wait_ge(x2_copied, 4 * s + 4)
                pe.sem_inc(pe_passed, 1)
                columns = x2[:].rearrange("r (g b) d -> r g (b d)", b=GROUP)
                for n in range(PER_BATCH):
                    mm = nc.tensor.transpose(bank[:, n * HIDDEN:(n + 1) * HIDDEN],
                                             columns[:, k * PER_BATCH + n, :], ident[0:HIDDEN, 0:HIDDEN])
                return mm

            def interact_groups(bank, s, k):
                pe.wait_ge(block_ready, 8 * s + 9)
                for n in range(PER_BATCH):
                    g = k * PER_BATCH + n
                    nc.tensor.matmul(bank[0:HIDDEN, n * BLOCK:(n + 1) * BLOCK],
                                     grouped_x2[:, g, :], block_x0[:, g, 0:1 + HALF_F, :],
                                     start=True, stop=True)
                    mm = nc.tensor.matmul(bank[HIDDEN:P, n * BLOCK + GROUP:(n + 1) * BLOCK],
                                          grouped_x2[:, g, :], block_x0[:, g, 1 + HALF_F:, :],
                                          start=True, stop=True)
                return mm

            def sum_z3(bank):
                for k in range(HALF_F):
                    half = k % 2
                    mm = nc.tensor.matmul(bank[half * HIDDEN:(half + 1) * HIDDEN, 0:P], w2_sb[:, k, :],
                                          inter[:, k, :], start=(k < 2), stop=(k >= HALF_F - 2))
                return mm

            def mlp1(bank, s, m):
                cols, units = bass.ts(s, P), slice(m * P, (m + 1) * P)
                if m == 0:
                    pe.wait_ge(z1_added, s + 1)
                    pe.wait_ge(z3_added, s + 1)
                nc.tensor.matmul(bank[:, 0:P], top1_z1_dense[:, units], z1_dense[:, cols],
                                 start=True, stop=False)
                return nc.tensor.matmul(bank[:, 0:P], top1_z23[:, units], z23[:, cols],
                                        start=False, stop=True)

            def mlp2(bank, m):
                for k in range(M1):
                    mm = nc.tensor.matmul(bank[:, 0:P], top2_sb[:, k, m * P:(m + 1) * P], hidden1[:, k, :],
                                          start=(k == 0), stop=(k == M1 - 1))
                return mm

            def mlp3(bank):
                for k in range(M2):
                    mm = nc.tensor.matmul(bank[0:1, 0:P], top3_sb[:, k:k + 1], hidden2[:, k, :],
                                          start=(k == 0), stop=(k == M2 - 1))
                return mm

            def step(s, name):
                number, bank, m = step_number(s, name), step_bank(s, name), int(name[1:] or 0)
                if in_end(s, name):
                    needed = {"I": f"T{m}", "Z": "I3", "B": "A3", "Y": "B1"}.get(name[0])
                    copied = [step_number(s, needed) + 3] if needed else []
                    if number < END_FIRST + 2:
                        copied.append(number + 1)
                    elif number >= END_FIRST + len(END_BANKS):
                        copied.append(number - len(END_BANKS) + 3)
                    if copied:
                        pe.wait_ge(step_copied, max(copied))
                else:
                    pe.wait_ge(step_copied, number + (2 if name in ("Z", "B0", "Y") else 1))
                if name[0] == "T":
                    mm = transpose_groups(bank, s, m)
                elif name[0] == "I":
                    mm = interact_groups(bank, s, m)
                elif name == "Z":
                    mm = sum_z3(bank)
                elif name[0] == "A":
                    mm = mlp1(bank, s, m)
                elif name[0] == "B":
                    mm = mlp2(bank, m)
                else:
                    mm = mlp3(bank)
                mm.then_inc(step_made, 1)

            def steps(s, place):
                for name in PLACES[place]:
                    step(s - 1, name)

            def first_tile():
                spread_x1(0, 0, 2)
                layer1(0, 1)
                layer2(0, 0, 0)
                spread_x1(0, 0, 3)
                layer2(0, 0, 1)
                transpose_x0(1, 1)
                spread_x1(0, 1, 0)
                layer2(0, 0, 2)
                spread_x1(0, 1, 1)
                layer2(0, 0, 3)
                spread_x1(0, 1, 2)
                spread_x1(0, 1, 3)
                layer2(0, 1, 0)
                layer2(0, 1, 1)
                pe.wait_ge(x0_t_copied, 1 + NI)
                layer1(1, 0)
                layer2(0, 1, 2)
                spread_x1(1, 0, 0)
                spread_x1(1, 0, 1)

            def tile(s, parity, last=False):
                if last:
                    layer2(s - 1, 1, 3)
                else:
                    layer2(s - 1, 1, 3, range(NI - 1))
                    transpose_x0(s + 1, 1 - parity)
                    layer2(s - 1, 1, 3, range(NI - 1, NI))
                spread_x1(s, 0, 2)
                if not last:
                    pe.wait_ge(x0_t_copied, s + 1 + NI)
                layer1(s, 1)
                steps(s, 0)
                layer2(s, 0, 0)
                spread_x1(s, 0, 3)
                steps(s, 1)
                layer2(s, 0, 1)
                steps(s, 2)
                spread_x1(s, 1, 0)
                spread_x1(s, 1, 1)
                layer2(s, 0, 2)
                steps(s, 3)
                spread_x1(s, 1, 2)
                layer2(s, 0, 3)
                steps(s, 4)
                if last:
                    spread_x1(s, 1, 3)
                    for j in range(NJ):
                        layer2(s, 1, j)
                else:
                    layer1(s + 1, 0)
                    layer2(s, 1, 0)
                    spread_x1(s, 1, 3)
                    steps(s, 5)
                    layer2(s, 1, 1)
                    steps(s, 6)
                    spread_x1(s + 1, 0, 0)
                    spread_x1(s + 1, 0, 1)
                    steps(s, 7)
                    layer2(s, 1, 2)
                    steps(s, 8)

            pe.wait_ge(loaded, LOADED)
            for i, bank in enumerate((x1_ps, x2_ps, group_ps[:, 0, :])):
                pe.wait_ge(gathered[0][i], rows_gathered(0, 0))
                nc.tensor.transpose(bank[:, 0:P], embedded[:, 0, i * P:(i + 1) * P], ident[:]
                                    ).then_inc(x0_transposed, 1)
            pe.wait_ge(w0_ready, 1)
            pe.wait_ge(x0_t_copied, NI)
            layer1(0, 0)
            pe.wait_ge(select_ready, 1)
            keep_warm(2)
            spread_x1(0, 0, 0)
            spread_x1(0, 0, 1)
            keep_warm(3)
            first_tile()
            with pe.Fori(0, TILES // 2 - 1) as n:
                tile(2 * n + 1, 1)
                tile(2 * n + 2, 0)
            tile(TILES - 1, 1, last=True)
            for s, name in END:
                step(s, name)

        @block.vector
        def _(dve):
            def square(s, c):
                head = isinstance(s, int) and s + c == 0
                if not head:
                    dve.wait_ge(by_g_loaded[c], 48 * s + 48 * c)
                for i in range(NI):
                    if head:
                        dve.wait_ge(head_loaded[i], 48)
                    else:
                        dve.wait_ge(by_f_loaded[c][i], 16 * s + 16 * c)
                    nc.vector.tensor_tensor(x0_by_g[:, c, i], x0_by_f[:, c, i], x0_by_g[:, c, i],
                                            ALU.mult).then_inc(squares_made, 1)

            def product(s, c, j):
                n = 8 * s + 4 * c + j
                dve.wait_ge(x1_spread, n + 1)
                if not (isinstance(s, int) and n < RING):
                    dve.wait_ge(products_used, n + 1 - RING)
                spread = x1_by_h[:, j % 2, :].unsqueeze(1).broadcast_to([P, NI, PAIR])
                nc.vector.tensor_tensor(products[:, j % RING], x0_by_f[:, c], spread,
                                        ALU.mult).then_inc(products_made, 1)

            def low_part(s, c):
                for u in range(2):
                    dve.wait_ge(x1_high, 4 * s + 2 * c + 1 + u)
                    here, there = slice(u * HIDDEN, (u + 1) * HIDDEN), slice((1 - u) * HIDDEN, (2 - u) * HIDDEN)
                    cols = slice(u * CHUNK, (u + 1) * CHUNK)
                    nc.vector.tensor_tensor(x1_split[there, c, cols], x1_ps[here, :], x1_split[here, c, cols],
                                            ALU.subtract).then_inc(x1_low, 1)

            def add_z1(s):
                dve.wait_ge(z1_moved, s + 1)
                nc.vector.tensor_tensor(z1_dense[0:HIDDEN, bass.ts(s, P)], z1[0:HIDDEN, bass.ts(s, P)],
                                        z1_upper[:], ALU.add).then_inc(z1_added, 1)

            def add_z3(s):
                dve.wait_ge(z3_moved, s + 1)
                nc.vector.tensor_tensor(z23[HIDDEN:P, bass.ts(s, P)], step_bank(s, "Z")[0:HIDDEN, 0:P],
                                        z3_upper[:], ALU.add).then_inc(z3_added, 1)

            def tile(s, last=False):
                for c in range(2):
                    nxt = (s, 1) if c == 0 else None if last else (s + 1, 0)
                    product(s, c, 0)
                    late = isinstance(s, int) and (s, c) == (0, 1)
                    if nxt and not late:
                        square(*nxt)
                    product(s, c, 1)
                    if c == 1 and not late:
                        add_z1(s - 1)
                        add_z3(s - 1)
                    product(s, c, 2)
                    if late:
                        square(*nxt)
                    elif nxt:
                        low_part(*nxt)
                    product(s, c, 3)
                    if late:
                        low_part(*nxt)

            dve.wait_ge(loaded, LOADED)
            nc.vector.tensor_tensor(w0_sb[HIDDEN:P], w0_sb[HIDDEN:P], w0_mirror_sb[HIDDEN:P],
                                    ALU.add).then_inc(w0_ready, 1)
            nc.vector.tensor_copy(select[:], select_f32).then_inc(select_ready, 1)
            square(0, 0)
            low_part(0, 0)
            tile(0)
            with dve.Fori(1, TILES - 1) as s:
                tile(s)
            tile(TILES - 1, last=True)
            add_z1(TILES - 1)
            add_z3(TILES - 1)

        @block.scalar
        def _(act):
            def copy_x0(s, parity):
                act.wait_ge(x0_stored, 48 * s + 32)
                act.wait_ge(x0_transposed, s + NI)
                nc.scalar.activation(x0_t[:], x0_bank(s)[:, 0:NI * P].rearrange("p (i b) -> p i b", i=NI),
                                     ACT.Copy).then_inc(x0_t_copied, 1)
                for i in range(NI):
                    act.wait_ge(gathered[parity][i], rows_gathered(s, parity))
                nc.scalar.activation(embedded_df[:], embedded[:, parity].rearrange("p (f d) -> p d f", d=DIM),
                                     ACT.Copy).then_inc(x0_permuted, 1)

            def high_part(s, c):
                act.wait_ge(x1_made, 2 * s + c + 1)
                if not (isinstance(s, int) and s == 0):
                    act.wait_ge(z1_step, 7 * s - 5 + 3 * c)
                    act.wait_ge(x1_spread, 8 * s - 4 + 4 * c)
                for u in range(2):
                    rows, cols = slice(u * HIDDEN, (u + 1) * HIDDEN), slice(u * CHUNK, (u + 1) * CHUNK)
                    nc.scalar.activation(x1_split[rows, c, cols], x1_ps[rows, :],
                                         ACT.Copy).then_inc(x1_high, 1)

            def copy_x2(s, c):
                act.wait_ge(products_used, 8 * s + 4 * c + 4)
                if c == 0 and not (isinstance(s, int) and s == 0):
                    act.wait_ge(step_made, step_number(s - 1, "T3") + 1)
                for u in range(2):
                    d0, dims = 8 * c + 4 * u, CHUNK // P
                    nc.scalar.activation(x2[:, :, d0:d0 + dims].rearrange("r b d -> r d b"),
                                         x2_ps[u * HIDDEN:(u + 1) * HIDDEN, :].rearrange("r (d b) -> r d b", d=dims),
                                         ACT.Copy).then_inc(x2_copied, 1)

            def block_diagonal(s, samples):
                act.wait_ge(x0_grouped, 16 * s + 16)
                for b in samples:
                    nc.scalar.activation(block_x0[:, :, 1:, b], grouped_x0[:], ACT.Copy,
                                         scale=sample_mask[:, b:b + 1]).then_inc(block_ready, 1)

            def load_groups(s, first=False):
                act.wait_ge(x0_stored, 48 * s + 80)
                if not first:
                    act.wait_ge(block_ready, 8 * s + 1)
                act.dma_start(grouped_x0[:], x0_groups[s].rearrange("(g b) d f -> (b d) g f", b=GROUP)
                              ).then_inc(x0_grouped, 16)

            def copy_groups(bank, s, k):
                return nc.scalar.activation(grouped_x2[:, k * PER_BATCH:(k + 1) * PER_BATCH, :],
                                            bank[:, 0:PER_BATCH * HIDDEN].rearrange(
                                                "p (n r) -> p n r", n=PER_BATCH), ACT.Copy)

            def copy_interactions(bank, s, k):
                first = k * PER_BATCH * GROUP
                block = bank[:, 0:PER_BATCH * BLOCK].rearrange("p (n t b) -> p t n b", n=PER_BATCH, b=GROUP)
                nc.scalar.activation(
                    z23[0:HIDDEN, bass.ds(s * P + first, PER_BATCH * GROUP)].rearrange(
                        "p (n b) -> p n b", n=PER_BATCH), block[0:HIDDEN, 0], ACT.Copy)
                return nc.scalar.activation(
                    inter[:, :, first:first + PER_BATCH * GROUP].rearrange("p t (n b) -> p t n b", n=PER_BATCH),
                    block[:, 1:], ACT.Copy)

            def move_z1(s):
                act.wait_ge(z1_step, 7 * s + 8)
                if not (isinstance(s, int) and s == 0):
                    act.wait_ge(z1_added, s)
                nc.scalar.activation(z1_upper[:], z1[HIDDEN:P, bass.ts(s, P)], ACT.Copy).then_inc(z1_moved, 1)

            def move_z3(bank, s):
                if not (isinstance(s, int) and s == 0):
                    act.wait_ge(z3_added, s)
                nc.scalar.activation(z3_upper[:], bank[HIDDEN:P, 0:P], ACT.Copy).then_inc(z3_moved, 1)
                act.wait_ge(z3_moved, s + 1)
                act.sem_inc(step_copied, 1)

            def relu(to, bank, bias, m):
                return nc.scalar.activation(to[:, m, :], bank[:, 0:P], ACT.Relu, bias=bias[:, m:m + 1])

            def copy_step(s, name):
                bank, m = step_bank(s, name), int(name[1:] or 0)
                act.wait_ge(step_made, step_number(s, name) + 1)
                if name[0] == "T":
                    copy_groups(bank, s, m).then_inc(step_copied, 1)
                elif name[0] == "I":
                    copy_interactions(bank, s, m).then_inc(step_copied, 1)
                elif name == "Z":
                    move_z3(bank, s)
                elif name[0] == "A":
                    relu(hidden1, bank, bias1, m).then_inc(step_copied, 1)
                elif name[0] == "B":
                    relu(hidden2, bank, bias2, m).then_inc(step_copied, 1)
                else:
                    nc.scalar.activation(y_row[:, bass.ts(s, P)], bank[0:1, 0:P],
                                         ACT.Copy).then_inc(step_copied, 1)

            def copies(s, place):
                if not (isinstance(s, int) and s == 0):
                    for name in PLACES[place]:
                        copy_step(s - 1, name)

            def tile(s, parity, last=False):
                first = isinstance(s, int) and s == 0
                load_groups(s, first)
                if first:
                    high_part(0, 1)
                    copy_x0(1, 1)
                else:
                    if not last:
                        copy_x0(s + 1, 1 - parity)
                    copy_x2(s - 1, 1)
                    high_part(s, 1)
                    copies(s, 0)
                copies(s, 1)
                copies(s, 2)
                copies(s, 3)
                if not first:
                    move_z1(s - 1)
                copy_x2(s, 0)
                copies(s, 4)
                block_diagonal(s, range(GROUP // 2))
                if not last:
                    high_part(s + 1, 0)
                block_diagonal(s, range(GROUP // 2, GROUP))
                if not last:
                    copies(s, 5)
                    copies(s, 6)
                    copies(s, 7)
                    copies(s, 8)

            act.wait_ge(loaded, LOADED)
            act.sem_inc(step_copied, 2)
            nc.scalar.activation(block_x0[:, :, 0, :], sample_mask[:].unsqueeze(1).broadcast_to([P, GROUPS, GROUP]),
                                 ACT.Copy).then_inc(block_ready, 1)
            for i, bank in enumerate((x1_ps, x2_ps, group_ps[:, 0, :])):
                act.wait_ge(x0_transposed, i + 1)
                nc.scalar.activation(x0_t[:, i, :], bank[:, 0:P], ACT.Copy).then_inc(x0_t_copied, 1)
            nc.scalar.activation(embedded_df[:], embedded[:, 0].rearrange("p (f d) -> p d f", d=DIM),
                                 ACT.Copy).then_inc(x0_permuted, 1)
            high_part(0, 0)
            tile(0, 0)
            with act.Fori(0, TILES // 2 - 1) as n:
                tile(2 * n + 1, 1)
                tile(2 * n + 2, 0)
            tile(TILES - 1, 1, last=True)
            copy_x2(LAST, 1)
            move_z1(LAST)
            for s, name in END:
                copy_step(s, name)
            act.wait_ge(step_copied, STEPS_MADE + 2)
            act.dma_start(out.rearrange("b o -> o b"), y_row[:]).then_inc(stored, 16)
            act.wait_ge(stored, 16)


def constants():
    identity = np.eye(P, dtype=np.float32)
    select_h = np.zeros((2, HIDDEN, NJ, HB, FB), np.float32)
    for j in range(NJ):
        for h in range(HB):
            select_h[:, HB * j + h, j, h, :] = 1.0
    same_sample = np.repeat(np.eye(GROUP, dtype=np.float32), DIM, axis=0)
    return identity, select_h.reshape(P, NJ, P), same_sample


def kernel(**inputs):
    import concourse.bacc as bacc
    from concourse.bass_utils import run_bass_kernel_spmd

    x = {k: np.asarray(v) for k, v in inputs.items()}
    identity, select_h, same_sample = constants()
    w0 = x["L0_rec_W0"].reshape(FEATURES, FEATURES, HIDDEN)
    w0_rows = np.stack([np.roll(w0, -FB * i, axis=1)[FB * i:FB * i + FB, 0:HB] for i in range(NI)])
    w0_back = np.stack([np.roll(w0, -FB * i, axis=0)[0:HB, FB * i:FB * i + FB] for i in range(NI)])
    w0_back[:, 0:FB] = 0.0
    arrays = {
        "ids": x["ids"].reshape(TILES, P, FEATURES),
        "w0": w0_rows.transpose(2, 1, 0, 3).reshape(P, NI, HIDDEN),
        "w0_mirror": w0_back.transpose(1, 2, 0, 3).reshape(P, NI, HIDDEN),
        "w1": x["L0_rec_W1"].reshape(NI, FB, NJ, HB, HIDDEN).transpose(3, 1, 2, 0, 4).reshape(P, NJ, NI, HIDDEN),
        "w2": x["L0_rec_W2"].reshape(2, HALF_F, HIDDEN, HIDDEN).transpose(0, 2, 1, 3).reshape(P, HALF_F, HIDDEN),
        "top1": x["W_top1"], "top1_bias": x["b_top1"].reshape(M1, P).T,
        "top2": x["W_top2"], "top2_bias": x["b_top2"].reshape(M2, P).T,
        "top3": x["W_top3"].reshape(M2, P).T, "dense_t": x["dense_ctx"].T,
        "identity": identity, "select_h": select_h, "same_sample": same_sample,
    }
    names = [f"tbl_{f}" for f in range(FEATURES)]
    arrays.update({n: x[n] for n in names})
    arrays = {f"in_{k}": np.ascontiguousarray(v) for k, v in arrays.items()}

    nc = bacc.Bacc("TRN2", target_bir_lowering=False, num_devices=1)
    aps = {k[3:]: nc.dram_tensor(k, v.shape, mybir.dt.from_np(v.dtype), kind="ExternalInput").ap()
           for k, v in arrays.items()}
    out = nc.dram_tensor("out_y", (BATCH, 1), F32, kind="ExternalOutput").ap()
    dlrm_cin_tower(nc, aps["ids"], [aps[n] for n in names], aps["w0"], aps["w0_mirror"], aps["w1"],
                   aps["w2"], aps["top1"], aps["top1_bias"], aps["top2"], aps["top2_bias"], aps["top3"],
                   aps["dense_t"], aps["identity"], aps["select_h"], aps["same_sample"], out)
    result = run_bass_kernel_spmd(nc, [arrays], core_ids=[0])
    return result.results[0]["out_y"]
```
